# Optimizing a Trainium2 kernel written in Bass

```python
import numpy as np
import jax
import jax.numpy as jnp

def _softmax(x, axis=-1):
    return jax.nn.softmax(x, axis=axis)

def _gelu(x):
    return jax.nn.gelu(x, approximate=True)

def _silu(x):
    return jax.nn.silu(x)

def _sigmoid(x):
    return jax.nn.sigmoid(x)

def _layernorm(x, axis=-1, eps=1e-05):
    m = jnp.mean(x, axis=axis, keepdims=True)
    v = jnp.var(x, axis=axis, keepdims=True)
    return (x - m) / jnp.sqrt(v + eps)

def _scatter_add(tgt, idx, src, axis=0):
    return tgt.at[idx].add(src)

def _segment_sum(src, seg, n):
    return jax.ops.segment_sum(src, seg, n)
kernel_name = 'mk_sandwich_d1_jaxref_r8_d33839'

def setup_inputs(seed: int=0):
    np.random.seed(seed)
    _w = jnp.asarray

    def _L0_attn_setup():
        import jax, jax.numpy as jnp
        import numpy as np
        D_MODEL = 256
        N_HEADS = 16
        D_K = D_MODEL // N_HEADS
        EPS = 1e-06
        key = jax.random.key(seed)
        ks = jax.random.split(key, 9)
        s = 1.0 / np.sqrt(D_MODEL)
        return {'x': jax.random.normal(ks[0], (4, 512, D_MODEL), dtype=jnp.float32), 'Wq': jax.random.normal(ks[1], (D_MODEL, D_MODEL), dtype=jnp.float32) * s, 'bq': jnp.zeros((D_MODEL,), dtype=jnp.float32), 'Wk': jax.random.normal(ks[2], (D_MODEL, D_MODEL), dtype=jnp.float32) * s, 'bk': jnp.zeros((D_MODEL,), dtype=jnp.float32), 'Wv': jax.random.normal(ks[3], (D_MODEL, D_MODEL), dtype=jnp.float32) * s, 'bv': jnp.zeros((D_MODEL,), dtype=jnp.float32), 'Wo': jax.random.normal(ks[4], (D_MODEL, D_MODEL), dtype=jnp.float32) * s, 'bo': jnp.zeros((D_MODEL,), dtype=jnp.float32)}
    _L0_attn_in = _L0_attn_setup()

    def _L0_ffn_setup():
        import jax, jax.numpy as jnp
        import numpy as np
        HIDDEN = 256
        INTER = 96
        NUM_EXPERTS = 32
        TOP_K = 8
        B, S = (1, 64)
        key = jax.random.key(seed)
        ks = jax.random.split(key, 5)
        scale_h = 1.0 / np.sqrt(HIDDEN)
        scale_i = 1.0 / np.sqrt(INTER)
        return {'hidden_states': jax.random.normal(ks[0], (B, S, HIDDEN), dtype=jnp.float32), 'gate_w': jax.random.normal(ks[1], (NUM_EXPERTS, HIDDEN), dtype=jnp.float32) * scale_h, 'gate_proj': jax.random.normal(ks[2], (NUM_EXPERTS, HIDDEN, INTER), dtype=jnp.float32) * scale_h, 'up_proj': jax.random.normal(ks[3], (NUM_EXPERTS, HIDDEN, INTER), dtype=jnp.float32) * scale_h, 'down_proj': jax.random.normal(ks[4], (NUM_EXPERTS, INTER, HIDDEN), dtype=jnp.float32) * scale_i}
    _L0_ffn_in = _L0_ffn_setup()
    _d = {'L0_attn_x': _L0_attn_in['x'], 'L0_attn_Wq': _L0_attn_in['Wq'], 'L0_attn_bq': _L0_attn_in['bq'], 'L0_attn_Wk': _L0_attn_in['Wk'], 'L0_attn_bk': _L0_attn_in['bk'], 'L0_attn_Wv': _L0_attn_in['Wv'], 'L0_attn_bv': _L0_attn_in['bv'], 'L0_attn_Wo': _L0_attn_in['Wo'], 'L0_attn_bo': _L0_attn_in['bo'], 'L0_ffn_gate_w': _L0_ffn_in['gate_w'], 'L0_ffn_gate_proj': _L0_ffn_in['gate_proj'], 'L0_ffn_up_proj': _L0_ffn_in['up_proj'], 'L0_ffn_down_proj': _L0_ffn_in['down_proj']}
    _x0 = _d['L0_attn_x']
    _d['L0_attn_x'] = jax.random.normal(jax.random.fold_in(jax.random.key(seed), 1), (2, 512, 256), dtype=_x0.dtype)
    del _x0
    return _d

def reference(L0_attn_x, L0_attn_Wq, L0_attn_bq, L0_attn_Wk, L0_attn_bk, L0_attn_Wv, L0_attn_bv, L0_attn_Wo, L0_attn_bo, L0_ffn_gate_w, L0_ffn_gate_proj, L0_ffn_up_proj, L0_ffn_down_proj):

    def _L0_attn_ref(x, Wq, bq, Wk, bk, Wv, bv, Wo, bo):
        import jax, jax.numpy as jnp
        import numpy as np
        D_MODEL = 256
        N_HEADS = 16
        D_K = D_MODEL // N_HEADS
        EPS = 1e-06
        b, n, _ = x.shape
        h, d = (N_HEADS, D_K)

        def proj(W, bias):
            y = jnp.einsum('bnm,dm->bnd', x, W) + bias
            return y.reshape(b, n, h, d).transpose(0, 2, 1, 3)
        Q = jax.nn.relu(proj(Wq, bq))
        K = jax.nn.relu(proj(Wk, bk))
        V = proj(Wv, bv)
        pos = jnp.arange(n, dtype=x.dtype)
        decay = jnp.exp(-pos / n)[None, None, :, None]
        Q = Q * decay
        K = K * decay
        KV = jnp.einsum('bhnd,bhne->bhde', K, V)
        Ksum = K.sum(axis=2)
        Z = 1.0 / (jnp.einsum('bhnd,bhd->bhn', Q, Ksum)[..., None] + EPS)
        out = jnp.einsum('bhnd,bhde->bhne', Q, KV) * Z
        out = out.transpose(0, 2, 1, 3).reshape(b, n, h * d)
        return jnp.einsum('bnm,dm->bnd', out, Wo) + bo

    def _L0_ffn_ref(hidden_states, gate_w, gate_proj, up_proj, down_proj):
        import jax, jax.numpy as jnp
        import numpy as np
        HIDDEN = 256
        INTER = 96
        NUM_EXPERTS = 32
        TOP_K = 8
        B, S = (1, 64)
        b, s, h = hidden_states.shape
        x = hidden_states.reshape(-1, h)
        t = x.shape[0]
        router_logits = x @ gate_w.T
        probs = jax.nn.softmax(router_logits, axis=-1)
        top_w, top_i = jax.lax.top_k(probs, TOP_K)
        top_w = top_w / jnp.sum(top_w, axis=-1, keepdims=True)
        comb = jnp.zeros((t, NUM_EXPERTS), dtype=x.dtype)
        comb = comb.at[jnp.arange(t)[:, None], top_i].add(top_w)
        g = jnp.einsum('th,ehi->eti', x, gate_proj)
        u = jnp.einsum('th,ehi->eti', x, up_proj)
        glu = jax.nn.silu(g) * u
        o = jnp.einsum('eti,eih->eth', glu, down_proj)
        y = jnp.einsum('eth,te->th', o, comb)
        return y.reshape(b, s, h)
    x = L0_attn_x
    x = x + _layernorm(_L0_attn_ref(_layernorm(x, axis=-1), L0_attn_Wq, L0_attn_bq, L0_attn_Wk, L0_attn_bk, L0_attn_Wv, L0_attn_bv, L0_attn_Wo, L0_attn_bo), axis=-1)
    x = x + _layernorm(_L0_ffn_ref(_layernorm(x, axis=-1), L0_ffn_gate_w, L0_ffn_gate_proj, L0_ffn_up_proj, L0_ffn_down_proj), axis=-1)
    return x

_drawn_inputs = setup_inputs


def setup_inputs(seed=0):
    import zlib

    import numpy as np

    out = dict(_drawn_inputs(seed))
    spreads = {'L0_attn_bq': (0.0, 0.1),
     'L0_attn_bk': (0.0, 0.1),
     'L0_attn_bv': (0.0, 0.1),
     'L0_attn_bo': (0.0, 0.1)}
    factors = {}
    for name, (base, spread) in spreads.items():
        noise = np.random.default_rng([zlib.crc32(name.encode()), seed]).standard_normal(out[name].shape)
        drawn = base * np.exp(spread * noise) if base else spread * noise
        out[name] = jnp.asarray(drawn.astype(out[name].dtype))
    for name, factor in factors.items():
        out[name] = (out[name] * factor).astype(out[name].dtype)
    return out
```

```python
from contextlib import ExitStack

import concourse.bass as bass
from concourse import mybir

F32 = mybir.dt.float32
F32R = mybir.dt.float32r
BF16 = mybir.dt.bfloat16
ALU = mybir.AluOpType
ACT = mybir.ActivationFunctionType
AX_X = mybir.AxisListType.X

P = 128
BATCHES = 2
TILES = 4
TOKENS = TILES * P
D_MODEL = 256
KD = D_MODEL // P
HEADS = 16
D_HEAD = D_MODEL // HEADS
HEADS_PART = HEADS // KD
NUM_WIDTH = P + HEADS_PART
EXPERTS = 32
INTER = 96
TOP_K = 8
SPLITS = 3
CHUNKS = EXPERTS * INTER // P
GU = 2 * KD * P
W_CHUNK = GU + D_MODEL
STEPS = BATCHES * CHUNKS
W_GROUPS = 6
GROUP = CHUNKS // W_GROUPS
LN_EPS = 1e-5
LOWEST = -3e38


def attention_moe_kernel(nc, x, w_qkvo, bias_q, bias_rows, gate_w, ffn_w, c_cols, c_mats, c_sel, out):
    with ExitStack() as ctx:
        def sb(name, shape, dt=F32):
            return ctx.enter_context(nc.sbuf_tensor(name, shape, dt))

        def sem(name):
            return ctx.enter_context(nc.semaphore(name))

        x_sb = sb("x_sb", [P, BATCHES, TILES, D_MODEL])
        w_att = sb("w_att", [P, KD, 4 * D_MODEL])
        bq_sb = sb("bq_sb", [P, KD])
        bias_sb = sb("bias_sb", [P, 3 * D_MODEL])
        gw_sb = sb("gw_sb", [P, KD, EXPERTS])
        w_raw = sb("w_raw", [P, CHUNKS, W_CHUNK])
        cols = sb("cols", [P, 2, TILES])
        mats = sb("mats", [P, 2 * P + HEADS_PART])
        sel = sb("sel", [SPLITS * EXPERTS, CHUNKS * P], BF16)
        ident = mats[:, 0:P]
        head_mask = mats[:, P:2 * P]
        head_cols = mats[:, 2 * P:2 * P + HEADS_PART]

        ident_bf = sb("ident_bf", [P, P], BF16)
        y_sb = sb("y_sb", [P, BATCHES, TILES, D_MODEL])
        yT = sb("yT", [P, BATCHES, KD, TOKENS])
        qT = sb("qT", [P, BATCHES, KD, TOKENS])
        kv = sb("kv", [P, BATCHES, TILES, D_MODEL + KD * (P + 1)])
        state = sb("state", [P, BATCHES, KD, NUM_WIDTH])
        den = sb("den", [P, BATCHES, TILES, KD, HEADS_PART])
        rden = sb("rden", [P, BATCHES, TILES, KD, HEADS_PART])
        att = sb("att", [P, BATCHES, TILES, D_MODEL])
        x1 = x_sb
        stats = sb("stats", [P, 8, TILES, 6])
        mv = sb("mv", [P, 8, TILES, 2])
        vareps = sb("vareps", [P, 8, TILES])
        rstd = sb("rstd", [P, 8, TILES])
        neg_half = sb("neg_half", [P, TILES])

        gwH = sb("gwH", [P, KD, EXPERTS], F32R)
        gwL = sb("gwL", [P, KD, EXPERTS], F32R)
        logits = sb("logits", [P, BATCHES, 2, TILES, EXPERTS])
        top8 = sb("top8", [P, BATCHES, TILES, TOP_K])
        shifted = sb("shifted", [P, BATCHES, 2, TILES, EXPERTS])
        expd = sb("expd", [P, BATCHES, 2, TILES, EXPERTS])
        chosen = sb("chosen", [P, BATCHES, TILES, EXPERTS])
        wsum = sb("wsum", [P, BATCHES, TILES])
        rsum = sb("rsum", [P, BATCHES, TILES])
        comb = sb("comb", [P, BATCHES, TILES, EXPERTS])
        rest = sb("rest", [P, BATCHES, 2, TILES, EXPERTS])
        parts = sb("parts", [P, BATCHES, TILES, SPLITS, EXPERTS], BF16)
        combT = sb("combT", [SPLITS * EXPERTS, BATCHES, TOKENS], BF16)

        zH = sb("zH", [P, BATCHES, KD, TOKENS], F32R)
        zL = sb("zL", [P, BATCHES, KD, TOKENS], F32R)
        guH = sb("guH", [P, 2, GU], F32R)
        guL = sb("guL", [P, 2, GU], F32R)
        dnH = sb("dnH", [P, 2, D_MODEL], F32R)
        dnL = sb("dnL", [P, 2, D_MODEL], F32R)
        glu = sb("glu", [P, 2, TOKENS])
        gluH = sb("gluH", [P, 2, TOKENS], F32R)
        gluL = sb("gluL", [P, 2, TOKENS], F32R)
        outT = yT
        moe = att

        psum = ctx.enter_context(nc.psum_tensor("psum", [P, 8, 512], F32))

        def bank(n):
            return psum[:, n, :]

        def a_bank(b, n):
            return psum[:, 4 * b + n, :]

        BANK_G, BANK_U, BANK_C, BANK_Y = 0, 2, 4, 6

        x_in = [sem(f"x_in{b}") for b in range(BATCHES)]
        watt_in = sem("watt_in")
        const_in = [sem(f"const_in{n}") for n in range(5)]
        sel_in = sem("sel_in")
        ffn_in = [sem(f"ffn_in{n}") for n in range(W_GROUPS)]
        out_done = sem("out_done")

        setup_dve = sem("setup_dve")
        setup_pool = sem("setup_pool")
        dve_local = sem("dve_local")
        pool_var = sem("pool_var")
        ln_var = sem("ln_var")
        ln_rstd = sem("ln_rstd")
        y_ready = sem("y_ready")
        yT_psum = sem("yT_psum")
        yT_ready = sem("yT_ready")
        q_psum = sem("q_psum")
        q_ready = sem("q_ready")
        kv_psum = sem("kv_psum")
        kv_biased = sem("kv_biased")
        k_ready = sem("k_ready")
        state_psum = sem("state_psum")
        state_ready = sem("state_ready")
        num_psum = sem("num_psum")
        o_ready = sem("o_ready")
        oT_psum = sem("oT_psum")
        oT_ready = sem("oT_ready")
        att_psum = sem("att_psum")
        att_biased = sem("att_biased")
        att_normed = sem("att_normed")
        x1_ready = sem("x1_ready")
        z_ready = sem("z_ready")
        zT_psum = sem("zT_psum")
        zH_ready = sem("zH_ready")
        zL_ready = sem("zL_ready")
        logits_psum = sem("logits_psum")
        shifted_ready = sem("shifted_ready")
        exp_ready = sem("exp_ready")
        parts_ready = sem("parts_ready")
        combT_psum = sem("combT_psum")
        combT_ready = sem("combT_ready")

        guH_ready = sem("guH_ready")
        guL_ready = sem("guL_ready")
        dnH_ready = sem("dnH_ready")
        dnL_ready = sem("dnL_ready")
        gate_psum = sem("gate_psum")
        up_psum = sem("up_psum")
        silu_ready = sem("silu_ready")
        weighted_ready = sem("weighted_ready")
        glu_ready = sem("glu_ready")
        gluH_ready = sem("gluH_ready")
        gluL_ready = sem("gluL_ready")
        down_psum = sem("down_psum")
        outT_ready = sem("outT_ready")
        moe_psum = sem("moe_psum")
        moe_ready = sem("moe_ready")
        moe_normed = sem("moe_normed")
        result_ready = sem("result_ready")

        block = ctx.enter_context(nc.Block())

        @block.sync
        def _(sp):
            def load_x(b):
                sp.dma_start(x_sb[:, b], x[b].rearrange("(t p) d -> p t d", p=P)).then_inc(x_in[b], 16)

            load_x(0)
            sp.dma_start(mats[:, :], c_mats).then_inc(const_in[0], 16)
            load_x(1)
            sp.dma_start(w_att[:, :, :], w_qkvo).then_inc(watt_in, 16)
            sp.dma_start(bq_sb[:, :], bias_q).then_inc(const_in[1], 16)
            sp.dma_start(bias_sb[:, :], bias_rows.partition_broadcast(P)).then_inc(const_in[2], 16)
            sp.dma_start(cols[:, :, :], c_cols).then_inc(const_in[3], 16)
            sp.dma_start(gw_sb[:, :, :], gate_w).then_inc(const_in[4], 16)
            sp.dma_start(sel[:, :], c_sel).then_inc(sel_in, 16)
            for g in range(W_GROUPS):
                sp.dma_start(w_raw[:, g * GROUP:(g + 1) * GROUP, :],
                             ffn_w[:, g * GROUP:(g + 1) * GROUP, :]).then_inc(ffn_in[g], 16)
            for b in range(BATCHES):
                sp.wait_ge(result_ready, TILES * (b + 1))
                sp.dma_start(out[b].rearrange("(t p) d -> p t d", p=P), moe[:, b]).then_inc(out_done, 16)
            sp.wait_ge(out_done, 16 * BATCHES)

        @block.gpsimd
        def _(pool):
            nc.gpsimd.memset(neg_half[:, :], -0.5).then_inc(setup_pool, 1)
            pool.wait_ge(setup_pool, 1)
            for n in range(8):
                pool.wait_ge(ln_var, n + 1)
                nc.gpsimd.tensor_tensor(rstd[:, n, :], vareps[:, n, :], neg_half[:, :], ALU.pow).then_inc(ln_rstd, 1)

        @block.tensor
        def _(pe):
            def product(dst, lhs, rhs, start=True, stop=True):
                return nc.tensor.matmul(dst, lhs, rhs, start=start, stop=stop)

            def split_product(dst, pairs, start=True, stop=True):
                n, last = 0, 3 * len(pairs) - 1
                for (lh, ll), (rh, rl) in pairs:
                    for a, c in ((lh, rh), (lh, rl), (ll, rh)):
                        mm = nc.tensor.matmul(dst, a, c, start=start and n == 0, stop=stop and n == last)
                        n += 1
                return mm

            def turn(src, b, first, ready, base, psum_sem):
                for k in range(KD):
                    for t in range(TILES):
                        if k == 0:
                            pe.wait_ge(ready, base + t + 1)
                        mm = nc.tensor.transpose(a_bank(b, first + k)[:, t * P:(t + 1) * P],
                                                 src[:, b, t, k * P:(k + 1) * P], ident)
                    mm.then_inc(psum_sem, 1)

            pe.wait_ge(const_in[0], 16)
            for b in range(BATCHES):
                turn(y_sb, b, 0, y_ready, TILES * b, yT_psum)

            pe.wait_ge(watt_in, 16)
            for b in range(BATCHES):
                pe.wait_ge(yT_ready, KD * (b + 1))
                for m in range(KD):
                    for k in range(KD):
                        mm = product(a_bank(b, 2 + m), w_att[:, k, m * P:(m + 1) * P], yT[:, b, k, :], k == 0, k == KD - 1)
                    mm.then_inc(q_psum, 1)

            for b in range(BATCHES):
                for t in range(TILES):
                    if t >= 2:
                        pe.wait_ge(kv_biased, TILES * b + t - 1)
                    for k in range(KD):
                        mm = product(a_bank(b, t % 2), yT[:, b, k, t * P:(t + 1) * P],
                                     w_att[:, k, D_MODEL:3 * D_MODEL], k == 0, k == KD - 1)
                    mm.then_inc(kv_psum, 1)

            for b in range(BATCHES):
                pe.wait_ge(q_ready, KD * (b + 1))
                for t in range(TILES):
                    pe.wait_ge(k_ready, TILES * b + t + 1)
                    for m in range(KD):
                        v0 = D_MODEL + m * (P + 1)
                        mm = product(a_bank(b, 2 + m)[:, 0:P + 1], kv[:, b, t, m * P:(m + 1) * P],
                                     kv[:, b, t, v0:v0 + P + 1], t == 0, t == TILES - 1)
                mm.then_inc(state_psum, 1)

            for b in range(BATCHES):
                pe.wait_ge(state_ready, b + 1)
                for t in range(TILES):
                    if t >= 2:
                        pe.wait_ge(o_ready, TILES * b + t - 1)
                    for m in range(KD):
                        mm = product(a_bank(b, t % 2)[:, m * NUM_WIDTH:(m + 1) * NUM_WIDTH],
                                     qT[:, b, m, t * P:(t + 1) * P], state[:, b, m, :])
                    mm.then_inc(num_psum, 1)

            for b in range(BATCHES):
                turn(y_sb, b, 2, o_ready, TILES * b, oT_psum)

            for b in range(BATCHES):
                pe.wait_ge(oT_ready, KD * (b + 1))
                for t in range(TILES):
                    for k in range(KD):
                        mm = product(a_bank(b, t // 2)[:, (t % 2) * D_MODEL:(t % 2 + 1) * D_MODEL],
                                     qT[:, b, k, t * P:(t + 1) * P], w_att[:, k, 3 * D_MODEL:4 * D_MODEL],
                                     k == 0, k == KD - 1)
                    mm.then_inc(att_psum, 1)

            for b in range(BATCHES):
                turn(y_sb, b, 2, z_ready, TILES * b, zT_psum)

            pe.wait_ge(setup_dve, 4)
            for b in range(BATCHES):
                pe.wait_ge(att_biased, TILES * (b + 1))
                pe.wait_ge(zL_ready, KD * (b + 1))
                for t in range(TILES):
                    r = slice(t * P, (t + 1) * P)
                    mm = split_product(a_bank(b, 0)[:, t * EXPERTS:(t + 1) * EXPERTS],
                                       [((zH[:, b, k, r], zL[:, b, k, r]), (gwH[:, k, :], gwL[:, k, :]))
                                        for k in range(KD)])
                mm.then_inc(logits_psum, 1)

            for b in range(BATCHES):
                pe.wait_ge(parts_ready, b + 1)
                turned = a_bank(b, 1)[0:SPLITS * EXPERTS, :].bitcast(BF16)
                for t in range(TILES):
                    mm = nc.tensor.transpose(turned[:, t * P:(t + 1) * P],
                                             parts[:, b, t].rearrange("p s e -> p (s e)"), ident_bf[:, :])
                mm.then_inc(combT_psum, 1)

            def gate_up(b, c, j, s):
                if not (isinstance(s, int) and s < 2):
                    pe.wait_ge(glu_ready, s - 1)
                pe.wait_ge(guL_ready, s + 1)
                product(bank(BANK_C + j), sel[:, bass.ts(c, P)], combT[:, b, :])
                for base, first, done in ((BANK_G, 0, gate_psum), (BANK_U, KD * P, up_psum)):
                    pairs = []
                    for k in range(KD):
                        r = slice(first + k * P, first + (k + 1) * P)
                        pairs.append(((guH[:, j, r], guL[:, j, r]), (zH[:, b, k, :], zL[:, b, k, :])))
                    split_product(bank(base + j), pairs).then_inc(done, 1)

            def down(j, s, start=False, stop=False):
                pe.wait_ge(gluL_ready, s + 1)
                pe.wait_ge(dnL_ready, s + 1)
                for m in range(KD):
                    r = slice(m * P, (m + 1) * P)
                    mm = split_product(bank(BANK_Y + m),
                                       [((dnH[:, j, r], dnL[:, j, r]), (gluH[:, j, :], gluL[:, j, :]))], start, stop)
                mm.then_inc(down_psum, 1)

            def turn_back(b):
                pe.wait_ge(outT_ready, KD * (b + 1))
                for t in range(TILES):
                    for k in range(KD):
                        mm = nc.tensor.transpose(
                            bank(BANK_Y + t // 2)[:, (t % 2) * D_MODEL + k * P:(t % 2) * D_MODEL + (k + 1) * P],
                            outT[:, b, k, t * P:(t + 1) * P], ident)
                    if t % 2:
                        mm.then_inc(moe_psum, 1)

            pe.wait_ge(sel_in, 16)
            pe.wait_ge(combT_ready, BATCHES)
            for b in range(BATCHES):
                s0 = b * CHUNKS
                gate_up(b, 0, 0, s0)
                if b > 0:
                    down(1, s0 - 1, stop=True)
                gate_up(b, 1, 1, s0 + 1)
                if b > 0:
                    turn_back(b - 1)
                    pe.wait_ge(moe_ready, 2 * b)
                down(0, s0, start=True)
                with pe.Fori(2, CHUNKS - 1, 2) as c:
                    for j in range(2):
                        gate_up(b, c + j, j, c + (s0 + j))
                        down(1 - j, c + (s0 + j - 1))
            down(1, STEPS - 1, stop=True)
            turn_back(BATCHES - 1)

        @block.scalar
        def _(act):
            act.wait_ge(const_in[1], 16)
            for b in range(BATCHES):
                for k in range(KD):
                    act.wait_ge(yT_psum, KD * b + k + 1)
                    nc.scalar.copy(yT[:, b, k, :], a_bank(b, k)).then_inc(yT_ready, 1)
            for b in range(BATCHES):
                for m in range(KD):
                    act.wait_ge(q_psum, KD * b + m + 1)
                    nc.scalar.activation(qT[:, b, m, :], a_bank(b, 2 + m), ACT.Relu,
                                         bias=bq_sb[:, m:m + 1]).then_inc(q_ready, 1)
            act.wait_ge(const_in[3], 16)
            for b in range(BATCHES):
                for t in range(TILES):
                    act.wait_ge(kv_biased, TILES * b + t + 1)
                    nc.scalar.activation(kv[:, b, t, 0:D_MODEL], kv[:, b, t, 0:D_MODEL], ACT.Relu,
                                         scale=cols[:, 0, t:t + 1]).then_inc(k_ready, 1)
            for b in range(BATCHES):
                for k in range(KD):
                    act.wait_ge(oT_psum, KD * b + k + 1)
                    nc.scalar.copy(qT[:, b, k, :], a_bank(b, 2 + k)).then_inc(oT_ready, 1)

            def split_gu(c, j, s):
                if not (isinstance(s, int) and s < 2):
                    act.wait_ge(up_psum, s - 1)
                nc.scalar.copy(guH[:, j, :], w_raw[:, c, 0:GU]).then_inc(guH_ready, 1)

            def split_dn(c, j, s):
                if not (isinstance(s, int) and s < 2):
                    act.wait_ge(down_psum, s - 1)
                nc.scalar.copy(dnH[:, j, :], w_raw[:, c, GU:W_CHUNK]).then_inc(dnH_ready, 1)

            act.wait_ge(ffn_in[0], 16)
            split_gu(0, 0, 0)
            split_gu(1, 1, 1)
            split_dn(0, 0, 0)

            for b in range(BATCHES):
                for k in range(KD):
                    act.wait_ge(zT_psum, KD * b + k + 1)
                    nc.scalar.copy(zH[:, b, k, :], a_bank(b, 2 + k)).then_inc(zH_ready, 1)
            for b in range(BATCHES):
                act.wait_ge(shifted_ready, b + 1)
                nc.scalar.activation(expd[:, b], shifted[:, b], ACT.Exp).then_inc(exp_ready, 1)
            for b in range(BATCHES):
                act.wait_ge(combT_psum, b + 1)
                nc.scalar.copy(combT[:, b, :],
                               a_bank(b, 1)[0:SPLITS * EXPERTS, 0:TOKENS // 2].bitcast(BF16)).then_inc(combT_ready, 1)

            def step(j, s, gu=None, dn=None):
                act.wait_ge(gate_psum, s + 1)
                if not (isinstance(s, int) and s < 2):
                    act.wait_ge(gluL_ready, s - 1)
                nc.scalar.activation(glu[:, j, :], bank(BANK_G + j), ACT.Silu).then_inc(silu_ready, 1)
                act.wait_ge(glu_ready, s + 1)
                if not (isinstance(s, int) and s < 2):
                    act.wait_ge(down_psum, s - 1)
                nc.scalar.copy(gluH[:, j, :], glu[:, j, :]).then_inc(gluH_ready, 1)
                if gu is not None:
                    split_gu(gu, j, s + 2)
                if dn is not None:
                    split_dn(dn, 1 - j, s + 1)

            def out_of_psum(b):
                act.wait_ge(down_psum, CHUNKS * (b + 1))
                for m in range(KD):
                    nc.scalar.copy(outT[:, b, m, :], bank(BANK_Y + m)).then_inc(outT_ready, 1)

            def moe_out(b):
                for n in range(TILES // 2):
                    act.wait_ge(moe_psum, 2 * b + n + 1)
                    nc.scalar.copy(moe[:, b, 2 * n:2 * n + 2, :],
                                   bank(BANK_Y + n).rearrange("p (t d) -> p t d", t=2)).then_inc(moe_ready, 1)

            for g in range(1, W_GROUPS):
                act.wait_ge(ffn_in[g], 16)
            for b in range(BATCHES):
                s0 = b * CHUNKS
                last = b == BATCHES - 1
                step(0, s0, 2, 1)
                if b > 0:
                    out_of_psum(b - 1)
                step(1, s0 + 1, 3)
                if b > 0:
                    moe_out(b - 1)
                split_dn(2, 0, s0 + 2)
                with act.Fori(2, CHUNKS - 3, 2) as c:
                    for j in range(2):
                        step(j, c + (s0 + j), c + (2 + j), c + (1 + j))
                step(0, s0 + CHUNKS - 2, None if last else 0, CHUNKS - 1)
                step(1, s0 + CHUNKS - 1, None if last else 1, None if last else 0)
            out_of_psum(BATCHES - 1)
            moe_out(BATCHES - 1)

        @block.vector
        def _(dve):
            local = [0]

            def own(ins):
                ins.then_inc(dve_local, 1)
                local[0] += 1
                return local[0]

            def ln_stats(n, src):
                for t in range(TILES):
                    v = own(nc.vector.bn_stats(stats[:, n, t, :], src[:, t, :]))
                dve.wait_ge(dve_local, v)
                for t in range(TILES):
                    v = own(nc.vector.bn_aggr(mv[:, n, t, :], stats[:, n, t, :]))
                dve.wait_ge(dve_local, v)
                nc.vector.tensor_scalar(vareps[:, n, :], mv[:, n, :, 1], LN_EPS, None, ALU.add).then_inc(ln_var, 1)

            def ln_apply(n, t, dst, src):
                return nc.vector.tensor_scalar(dst, src, mv[:, n, t, 0:1], rstd[:, n, t:t + 1],
                                               ALU.subtract, ALU.mult)

            for b in range(BATCHES):
                dve.wait_ge(x_in[b], 16)
                ln_stats(b, x_sb[:, b])
            for b in range(BATCHES):
                dve.wait_ge(ln_rstd, b + 1)
                for t in range(TILES):
                    ln_apply(b, t, y_sb[:, b, t, :], x_sb[:, b, t, :]).then_inc(y_ready, 1)

            for m in range(KD):
                v1 = D_MODEL + m * (P + 1) + P
                nc.vector.memset(kv[:, :, :, v1:v1 + 1], 1.0).then_inc(setup_dve, 1)
            dve.wait_ge(const_in[0], 16)
            dve.wait_ge(const_in[4], 16)
            gw = own(nc.vector.tensor_copy(gwH[:, :, :], gw_sb[:, :, :]))
            nc.vector.tensor_copy(ident_bf[:, :], ident).then_inc(setup_dve, 1)
            dve.wait_ge(dve_local, gw)
            nc.vector.tensor_tensor(gwL[:, :, :], gw_sb[:, :, :], gwH[:, :, :], ALU.subtract).then_inc(setup_dve, 1)

            dve.wait_ge(const_in[2], 16)
            for b in range(BATCHES):
                for t in range(TILES):
                    dve.wait_ge(kv_psum, TILES * b + t + 1)
                    own(nc.vector.tensor_tensor(
                        kv[:, b, t, D_MODEL:].rearrange("p (m e) -> p m e", m=KD)[:, :, 0:P],
                        a_bank(b, t % 2)[:, D_MODEL:].rearrange("p (m e) -> p m e", m=KD),
                        bias_sb[:, D_MODEL:2 * D_MODEL].rearrange("p (m e) -> p m e", m=KD), ALU.add))
                    nc.vector.tensor_tensor(kv[:, b, t, 0:D_MODEL], a_bank(b, t % 2)[:, 0:D_MODEL],
                                            bias_sb[:, 0:D_MODEL], ALU.add).then_inc(kv_biased, 1)

            for b in range(BATCHES):
                dve.wait_ge(state_psum, b + 1)
                for m in range(KD):
                    v = own(nc.vector.tensor_tensor(state[:, b, m, 0:P], a_bank(b, 2 + m)[:, 0:P], head_mask, ALU.mult))
                for m in range(KD):
                    ins = nc.vector.tensor_scalar(state[:, b, m, P:], head_cols, a_bank(b, 2 + m)[:, P:P + 1],
                                                  None, ALU.mult)
                    if m == 0:
                        own(ins)
                ins.then_inc(state_ready, 1)

            dve.wait_ge(const_in[3], 16)
            for b in range(BATCHES):
                for t in range(TILES):
                    dve.wait_ge(num_psum, TILES * b + t + 1)
                    both = a_bank(b, t % 2)[:, 0:KD * NUM_WIDTH].rearrange("p (m w) -> p m w", m=KD)
                    v = own(nc.vector.tensor_scalar(den[:, b, t], both[:, :, P:], cols[:, 1, t:t + 1], None, ALU.add))
                    dve.wait_ge(dve_local, v)
                    v = own(nc.vector.reciprocal(rden[:, b, t], den[:, b, t]))
                    dve.wait_ge(dve_local, v)
                    for m in range(KD):
                        ins = nc.vector.tensor_tensor(
                            y_sb[:, b, t, m * P:(m + 1) * P].rearrange("p (h e) -> p h e", e=D_HEAD),
                            both[:, m, 0:P].rearrange("p (h e) -> p h e", e=D_HEAD),
                            rden[:, b, t, m, :].unsqueeze(2).to_broadcast([P, HEADS_PART, D_HEAD]), ALU.mult)
                        if m == 0:
                            own(ins)
                    ins.then_inc(o_ready, 1)

            for b in range(BATCHES):
                for t in range(TILES):
                    dve.wait_ge(att_psum, TILES * b + 2 * (t // 2) + 2)
                    nc.vector.tensor_tensor(att[:, b, t, :], a_bank(b, t // 2)[:, (t % 2) * D_MODEL:(t % 2 + 1) * D_MODEL],
                                            bias_sb[:, 2 * D_MODEL:], ALU.add).then_inc(att_biased, 1)
                dve.wait_ge(att_biased, TILES * (b + 1))
                ln_stats(2 + b, att[:, b])
            for b in range(BATCHES):
                dve.wait_ge(ln_rstd, 3 + b)
                for t in range(TILES):
                    ln_apply(2 + b, t, att[:, b, t, :], att[:, b, t, :]).then_inc(att_normed, 1)
                for t in range(TILES):
                    dve.wait_ge(att_normed, TILES * b + t + 1)
                    nc.vector.tensor_tensor(x1[:, b, t, :], att[:, b, t, :], x_sb[:, b, t, :], ALU.add).then_inc(x1_ready, 1)
                dve.wait_ge(x1_ready, TILES * (b + 1))
                ln_stats(4 + b, x1[:, b])
            for b in range(BATCHES):
                dve.wait_ge(ln_rstd, 5 + b)
                dve.wait_ge(oT_psum, KD * (b + 1))
                for t in range(TILES):
                    ln_apply(4 + b, t, y_sb[:, b, t, :], x1[:, b, t, :]).then_inc(z_ready, 1)

            def low_gu(c, j, s):
                dve.wait_ge(guH_ready, s + 1)
                nc.vector.tensor_tensor(guL[:, j, :], w_raw[:, c, 0:GU], guH[:, j, :], ALU.subtract).then_inc(guL_ready, 1)

            def low_dn(c, j, s):
                dve.wait_ge(dnH_ready, s + 1)
                nc.vector.tensor_tensor(dnL[:, j, :], w_raw[:, c, GU:W_CHUNK], dnH[:, j, :],
                                        ALU.subtract).then_inc(dnL_ready, 1)

            low_gu(0, 0, 0)
            low_gu(1, 1, 1)
            low_dn(0, 0, 0)
            for b in range(BATCHES):
                for k in range(KD):
                    dve.wait_ge(zH_ready, KD * b + k + 1)
                    nc.vector.tensor_tensor(zL[:, b, k, :], a_bank(b, 2 + k), zH[:, b, k, :].bitcast(F32),
                                            ALU.subtract).then_inc(zL_ready, 1)

            for b in range(BATCHES):
                dve.wait_ge(logits_psum, b + 1)
                v = own(nc.vector.tensor_copy(logits[:, b, 0],
                                              a_bank(b, 0)[:, 0:TILES * EXPERTS].rearrange("p (t e) -> p t e", t=TILES)))
                dve.wait_ge(dve_local, v)
                for t in range(TILES):
                    v = own(nc.vector.max(top8[:, b, t, :], logits[:, b, 0, t, :]))
                dve.wait_ge(dve_local, v)
                for t in range(TILES):
                    v = own(nc.vector.match_replace(logits[:, b, 1, t, :], top8[:, b, t, :], logits[:, b, 0, t, :], LOWEST))
                dve.wait_ge(dve_local, v)
                for n in range(2):
                    ins = nc.vector.tensor_tensor(shifted[:, b, n], logits[:, b, n],
                                                  top8[:, b, :, 0:1].to_broadcast([P, TILES, EXPERTS]), ALU.subtract)
                    if n == 0:
                        own(ins)
                ins.then_inc(shifted_ready, 1)
            for b in range(BATCHES):
                dve.wait_ge(exp_ready, b + 1)
                v = own(nc.vector.tensor_tensor(chosen[:, b], expd[:, b, 0], expd[:, b, 1], ALU.subtract))
                dve.wait_ge(dve_local, v)
                v = own(nc.vector.tensor_reduce(wsum[:, b, :], chosen[:, b], AX_X, ALU.add))
                dve.wait_ge(dve_local, v)
                v = own(nc.vector.reciprocal(rsum[:, b, :], wsum[:, b, :]))
                dve.wait_ge(dve_local, v)
                v = own(nc.vector.tensor_tensor(comb[:, b], chosen[:, b],
                                                rsum[:, b, :].unsqueeze(2).to_broadcast([P, TILES, EXPERTS]), ALU.mult))
                dve.wait_ge(dve_local, v)
                left = comb[:, b]
                for n in range(SPLITS):
                    ins = nc.vector.tensor_copy(parts[:, b, :, n, :], left)
                    if n == SPLITS - 1:
                        ins.then_inc(parts_ready, 1)
                        break
                    dve.wait_ge(dve_local, own(ins))
                    v = own(nc.vector.tensor_tensor(rest[:, b, n], left, parts[:, b, :, n, :], ALU.subtract))
                    dve.wait_ge(dve_local, v)
                    left = rest[:, b, n]

            def step(j, s, gu=None, dn=None):
                dve.wait_ge(silu_ready, s + 1)
                nc.vector.tensor_tensor(glu[:, j, :], bank(BANK_C + j), glu[:, j, :], ALU.mult).then_inc(weighted_ready, 1)
                dve.wait_ge(up_psum, s + 1)
                dve.wait_ge(weighted_ready, s + 1)
                nc.vector.tensor_tensor(glu[:, j, :], bank(BANK_U + j), glu[:, j, :], ALU.mult).then_inc(glu_ready, 1)
                dve.wait_ge(gluH_ready, s + 1)
                nc.vector.tensor_tensor(gluL[:, j, :], glu[:, j, :], gluH[:, j, :], ALU.subtract).then_inc(gluL_ready, 1)
                if gu is not None:
                    low_gu(gu, j, s + 2)
                if dn is not None:
                    low_dn(dn, 1 - j, s + 1)

            def finish(b):
                n = 6 + b
                dve.wait_ge(moe_ready, 2 * (b + 1))
                ln_stats(n, moe[:, b])
                dve.wait_ge(ln_rstd, n + 1)
                for t in range(TILES):
                    ln_apply(n, t, moe[:, b, t, :], moe[:, b, t, :]).then_inc(moe_normed, 1)
                for t in range(TILES):
                    dve.wait_ge(moe_normed, TILES * b + t + 1)
                    nc.vector.tensor_tensor(moe[:, b, t, :], moe[:, b, t, :], x1[:, b, t, :], ALU.add).then_inc(result_ready, 1)

            for b in range(BATCHES):
                s0 = b * CHUNKS
                last = b == BATCHES - 1
                step(0, s0, 2, 1)
                step(1, s0 + 1, 3, 2)
                if b > 0:
                    finish(b - 1)
                with dve.Fori(2, CHUNKS - 3, 2) as c:
                    for j in range(2):
                        step(j, c + (s0 + j), c + (2 + j), c + (1 + j))
                step(0, s0 + CHUNKS - 2, None if last else 0, CHUNKS - 1)
                step(1, s0 + CHUNKS - 1, None if last else 1, None if last else 0)
            finish(BATCHES - 1)


def kernel(L0_attn_x, L0_attn_Wq, L0_attn_bq, L0_attn_Wk, L0_attn_bk, L0_attn_Wv, L0_attn_bv, L0_attn_Wo,
           L0_attn_bo, L0_ffn_gate_w, L0_ffn_gate_proj, L0_ffn_up_proj, L0_ffn_down_proj):
    import ml_dtypes as _ml
    import numpy as _np
    import concourse.bacc as _bacc
    from concourse import mybir as _mybir
    from concourse.bass_utils import run_bass_kernel_spmd as _run

    def rows_first(w):
        w = _np.asarray(w)
        return w.reshape(KD, P, w.shape[1]).transpose(1, 0, 2)

    def by_chunk(w):
        w = _np.asarray(w).transpose(1, 0, 2).reshape(KD, P, CHUNKS, P)
        return w.transpose(1, 2, 0, 3).reshape(P, CHUNKS, KD * P)

    down = _np.asarray(L0_ffn_down_proj).reshape(CHUNKS, P, D_MODEL).transpose(1, 0, 2)

    pos = _np.arange(TOKENS, dtype=_np.float32)
    decay = _np.exp(-pos / _np.float32(TOKENS)).reshape(TILES, P).T
    head = _np.arange(P) // D_HEAD
    mats = _np.concatenate([_np.eye(P), head[:, None] == head[None, :],
                            head[:, None] == _np.arange(HEADS_PART)[None, :]], axis=1).astype(_np.float32)
    inner = _np.arange(CHUNKS * P) // INTER
    sel = (_np.arange(SPLITS * EXPERTS)[:, None] % EXPERTS == inner[None, :]).astype(_ml.bfloat16)

    arrays = {
        "x": L0_attn_x,
        "w_qkvo": _np.concatenate([rows_first(_np.asarray(w).T) for w in (L0_attn_Wq, L0_attn_Wk, L0_attn_Wv, L0_attn_Wo)], axis=2),
        "bias_q": _np.asarray(L0_attn_bq).reshape(KD, P).T,
        "bias_rows": _np.concatenate([_np.asarray(v) for v in (L0_attn_bk, L0_attn_bv, L0_attn_bo)]),
        "gate_w": rows_first(_np.asarray(L0_ffn_gate_w).T),
        "ffn_w": _np.concatenate([by_chunk(L0_ffn_gate_proj), by_chunk(L0_ffn_up_proj), down], axis=2),
        "c_cols": _np.stack([decay, _np.float32(1e-6) / decay], axis=1).astype(_np.float32),
        "c_mats": mats,
        "c_sel": sel,
    }
    nc = _bacc.Bacc("TRN2", target_bir_lowering=False, num_devices=1)
    feed, args = {}, []
    for name, a in arrays.items():
        a = _np.ascontiguousarray(a)
        feed[f"in_{name}"] = a
        args.append(nc.dram_tensor(f"in_{name}", a.shape, _mybir.dt.from_np(a.dtype), kind="ExternalInput").ap())
    out = nc.dram_tensor("out", (BATCHES, TOKENS, D_MODEL), F32, kind="ExternalOutput").ap()
    attention_moe_kernel(nc, *args, out)
    return _run(nc, [feed], core_ids=[0]).results[0]["out"]
```

```python
from contextlib import ExitStack

import concourse.bass as bass
from concourse import mybir

F32 = mybir.dt.float32
F32R = mybir.dt.float32r
BF16 = mybir.dt.bfloat16
ALU = mybir.AluOpType
ACT = mybir.ActivationFunctionType
AX_X = mybir.AxisListType.X

P = 128
BATCHES = 2
TILES = 4
TOKENS = TILES * P
D_MODEL = 256
KD = D_MODEL // P
HEADS = 16
D_HEAD = D_MODEL // HEADS
HEADS_PART = HEADS // KD
NUM_WIDTH = P + HEADS_PART
EXPERTS = 32
INTER = 96
TOP_K = 8
SPLITS = 3
CHUNKS = EXPERTS * INTER // P
GU = 2 * KD * P
W_CHUNK = GU + D_MODEL
STEPS = BATCHES * CHUNKS
GROUPS = EXPERTS // 4
W_GROUPS = 6
GROUP = CHUNKS // W_GROUPS
NORMS = 4 * BATCHES
LN_ATT, LN_X1, LN_MOE = (2, 4), (3, 5), (6, 7)
LN_EPS = 1e-5
QKV = 3 * D_MODEL
FRONT, BACK = (0, 1), (2, 3)
LOWEST = -3e38


def attention_moe_kernel(nc, x, w_qkvo, bias_q, bias_rows, gate_w, ffn_w, c_cols, c_mats, c_sel, out):
    with ExitStack() as ctx:
        def sb(name, shape, dt=F32):
            return ctx.enter_context(nc.sbuf_tensor(name, shape, dt))

        def sem(name):
            return ctx.enter_context(nc.semaphore(name))

        x_sb = sb("x_sb", [P, BATCHES, TILES, D_MODEL])
        w_att = sb("w_att", [P, KD, 4 * D_MODEL])
        bq_sb = sb("bq_sb", [P, KD])
        bias_sb = sb("bias_sb", [P, 3 * D_MODEL])
        gw_sb = sb("gw_sb", [P, KD, P])
        w_raw = sb("w_raw", [P, CHUNKS, W_CHUNK])
        cols = sb("cols", [P, 2, TILES])
        mats = sb("mats", [P, 2 * P + HEADS_PART])
        sel = sb("sel", [SPLITS * EXPERTS, GROUPS * P], BF16)
        ident = mats[:, 0:P]
        head_mask = mats[:, P:2 * P]
        head_cols = mats[:, 2 * P:2 * P + HEADS_PART]

        ident_bf = sb("ident_bf", [P, P], BF16)
        y_sb = sb("y_sb", [P, BATCHES, TILES, D_MODEL])
        turned = sb("turned", [P, 2, BATCHES, KD, TOKENS])
        qT = turned[:, 1]
        kv = sb("kv", [P, BATCHES, TILES, 2 * KD, P + 1])
        state = sb("state", [P, BATCHES, KD, NUM_WIDTH])
        den = sb("den", [P, BATCHES, TILES, KD, HEADS_PART])
        rden = sb("rden", [P, BATCHES, TILES, KD, HEADS_PART])
        att = sb("att", [P, BATCHES, TILES, D_MODEL])
        x1 = x_sb
        stats = sb("stats", [P, NORMS, TILES, 6])
        mv = sb("mv", [P, NORMS, TILES, 2])
        vareps = sb("vareps", [P, NORMS, TILES])
        rstd = sb("rstd", [P, NORMS, TILES])
        shift = sb("shift", [P, NORMS, TILES])
        neg_half = sb("neg_half", [P, TILES])
        scratch = sb("scratch", [P, TILES])
        zeros = sb("zeros", [P, 512], BF16)

        gwH = sb("gwH", [P, KD, P], F32R)
        gwL = sb("gwL", [P, KD, P], F32R)
        top8 = sb("top8", [P, BATCHES, TILES, TOP_K])
        others = sb("others", [P, BATCHES, TILES, EXPERTS])
        shifted = sb("shifted", [P, BATCHES, 2, TILES, EXPERTS])
        expd = sb("expd", [P, BATCHES, 2, TILES, EXPERTS])
        chosen = sb("chosen", [P, BATCHES, TILES, EXPERTS])
        wsum = sb("wsum", [P, BATCHES, TILES])
        rsum = sb("rsum", [P, BATCHES, TILES])
        comb = sb("comb", [P, BATCHES, TILES, EXPERTS])
        rest = sb("rest", [P, BATCHES, 2, TILES, EXPERTS])
        parts = sb("parts", [P, BATCHES, TILES, SPLITS, EXPERTS], BF16)
        combT = sb("combT", [SPLITS * EXPERTS, BATCHES, TOKENS], BF16)

        zH = sb("zH", [P, BATCHES, KD, TOKENS], F32R)
        zL = sb("zL", [P, BATCHES, KD, TOKENS], F32R)
        guH = sb("guH", [P, 2, GU], F32R)
        guL = sb("guL", [P, 2, GU], F32R)
        glu = sb("glu", [P, 2, TOKENS])
        split = sb("split", [P, 2 * KD * QKV], F32R)
        wH = split[:, 0:KD * QKV].rearrange("p (k c) -> p k c", k=KD)
        wL = split[:, KD * QKV:].rearrange("p (k c) -> p k c", k=KD)
        gluH = split[:, 0:2 * TOKENS].rearrange("p (j t) -> p j t", j=2)
        gluL = split[:, 2 * TOKENS:4 * TOKENS].rearrange("p (j t) -> p j t", j=2)
        dnH = split[:, 4 * TOKENS:4 * TOKENS + 2 * D_MODEL].rearrange("p (j c) -> p j c", j=2)
        dnL = split[:, 4 * TOKENS + 2 * D_MODEL:4 * TOKENS + 4 * D_MODEL].rearrange("p (j c) -> p j c", j=2)
        weight_tiles = [
            turned[:, :].rearrange("p a b k t -> p (a b k) t"),
            kv[:, :].rearrange("p b t m c -> p (b t m c)")[:, 0:GROUPS * TOKENS].rearrange("p (g t) -> p g t", g=GROUPS),
        ]
        outT = turned[:, 0]
        moe = att

        psum = ctx.enter_context(nc.psum_tensor("psum", [P, 8, 512], F32))

        def bank(n):
            return psum[:, n, :]

        def a_bank(b, n):
            return psum[:, 4 * b + n, :]

        def logits_T(b):
            return y_sb[0:EXPERTS, b].rearrange("p t d -> p (t d)")[:, 0:TOKENS]

        BANK_G, BANK_U, BANK_Y, BANK_FREE = 0, 2, 4, 6
        BANK_LOGITS, BANK_TURNED_LOGITS, BANK_COMB = 6, 7, 6
        ATT_BANKS = ((0, 1, 2, 3), (4, 4, 1, 1))
        MOE_BANKS = ((6, 6, 7, 7), (0, 1, 2, 3))

        def banks_done(banks, b, t):
            return (len(set(banks[0])) if b else 0) + len(set(banks[b][:t + 1]))

        def last_in_bank(banks, b, t):
            return t == TILES - 1 or banks[b][t + 1] != banks[b][t]

        FIRST = 14
        WARM_START, WARM_Y = 20, 6

        x_in = [[sem(f"x_in{b}_{h}") for h in range(2)] for b in range(BATCHES)]
        wq_in = sem("wq_in")
        wkv_in = sem("wkv_in")
        wo_in = sem("wo_in")
        mats_in = sem("mats_in")
        bq_in = sem("bq_in")
        bias_in = sem("bias_in")
        cols_in = sem("cols_in")
        gw_in = sem("gw_in")
        sel_in = sem("sel_in")
        ffn_in = [sem(f"ffn_in{n}") for n in range(W_GROUPS)]
        out_done = sem("out_done")

        gw_zeroed = sem("gw_zeroed")
        zeroed = sem("zeroed")
        setup_dve = sem("setup_dve")
        setup_pool = sem("setup_pool")
        dve_local = sem("dve_local")
        ln_var = sem("ln_var")
        ln_rstd = sem("ln_rstd")
        shift_ready = sem("shift_ready")
        y_front = sem("y_front")
        y_back = sem("y_back")
        wqH_ready = sem("wqH_ready")
        wqL_ready = sem("wqL_ready")
        wkvH_ready = sem("wkvH_ready")
        wkL_ready = sem("wkL_ready")
        wvL_ready = sem("wvL_ready")
        yT_psum = sem("yT_psum")
        yH_ready = sem("yH_ready")
        yL_ready = sem("yL_ready")
        q_psum = sem("q_psum")
        q_ready = sem("q_ready")
        kv_psum = sem("kv_psum")
        kv_biased = sem("kv_biased")
        k_ready = sem("k_ready")
        state_psum = sem("state_psum")
        state_ready = sem("state_ready")
        num_psum = sem("num_psum")
        o_ready = sem("o_ready")
        oT_psum = sem("oT_psum")
        oT_ready = sem("oT_ready")
        att_psum = sem("att_psum")
        att_biased = sem("att_biased")
        att_front = sem("att_front")
        att_back = sem("att_back")
        x1_ready = sem("x1_ready")
        z_front = sem("z_front")
        z_back = sem("z_back")
        zT_psum = sem("zT_psum")
        zH_ready = sem("zH_ready")
        zL_ready = sem("zL_ready")
        logits_psum = sem("logits_psum")
        logits_ready = sem("logits_ready")
        turned_psum = sem("turned_psum")
        shifted_ready = sem("shifted_ready")
        exp_ready = sem("exp_ready")
        parts_ready = sem("parts_ready")
        combT_psum = sem("combT_psum")
        combT_ready = sem("combT_ready")
        weights_psum = sem("weights_psum")
        weights_ready = sem("weights_ready")

        guH_ready = sem("guH_ready")
        guL_ready = sem("guL_ready")
        dnH_ready = sem("dnH_ready")
        dnL_ready = sem("dnL_ready")
        gate_psum = sem("gate_psum")
        up_psum = sem("up_psum")
        silu_ready = sem("silu_ready")
        first_product = sem("first_product")
        glu_ready = sem("glu_ready")
        gluH_ready = sem("gluH_ready")
        gluL_ready = sem("gluL_ready")
        down_psum = sem("down_psum")
        outT_ready = sem("outT_ready")
        moe_psum = sem("moe_psum")
        moe_front = sem("moe_front")
        moe_back = sem("moe_back")
        result_ready = sem("result_ready")

        def rows(buf, b):
            return [buf[:, b, t, :] for t in range(TILES)]

        def moe_rows(b):
            two = len(set(MOE_BANKS[b])) < TILES
            return [bank(n)[:, (t % 2) * D_MODEL:(t % 2 + 1) * D_MODEL] if two else bank(n)[:, 0:D_MODEL]
                    for t, n in enumerate(MOE_BANKS[b])]

        block = ctx.enter_context(nc.Block())

        @block.sync
        def _(sp):
            def load_x(b):
                rows = x[b].rearrange("(t p) d -> p t d", p=P)
                for h in range(2):
                    tiles = slice(2 * h, 2 * h + 2)
                    sp.dma_start(x_sb[:, b, tiles], rows[:, tiles]).then_inc(x_in[b][h], 16)

            load_x(0)
            sp.dma_start(mats[:, :], c_mats).then_inc(mats_in, 16)
            sp.dma_start(w_att[:, :, D_MODEL:QKV], w_qkvo[:, :, D_MODEL:QKV]).then_inc(wkv_in, 16)
            sp.dma_start(w_att[:, :, 0:D_MODEL], w_qkvo[:, :, 0:D_MODEL]).then_inc(wq_in, 16)
            sp.dma_start(bq_sb[:, :], bias_q).then_inc(bq_in, 16)
            sp.dma_start(cols[:, :, :], c_cols).then_inc(cols_in, 16)
            load_x(1)
            sp.dma_start(bias_sb[:, :], bias_rows.partition_broadcast(P)).then_inc(bias_in, 16)
            sp.dma_start(w_att[:, :, QKV:], w_qkvo[:, :, QKV:]).then_inc(wo_in, 16)
            sp.wait_ge(gw_zeroed, 1)
            sp.dma_start(gw_sb[:, :, 0:EXPERTS], gate_w).then_inc(gw_in, 16)
            sp.dma_start(sel[:, :], c_sel).then_inc(sel_in, 16)
            for g in range(W_GROUPS):
                sp.dma_start(w_raw[:, g * GROUP:(g + 1) * GROUP, :],
                             ffn_w[:, g * GROUP:(g + 1) * GROUP, :]).then_inc(ffn_in[g], 16)
            for b in range(BATCHES):
                rows = out[b].rearrange("(t p) d -> p t d", p=P)
                for t in range(TILES):
                    sp.wait_ge(result_ready, TILES * b + t + 1)
                    sp.dma_start(rows[:, t, :], moe[:, b, t, :]).then_inc(out_done, 16)
            sp.wait_ge(out_done, 16 * BATCHES * TILES)

        @block.gpsimd
        def _(pool):
            nc.gpsimd.memset(gw_sb[:, :, :], 0.0).then_inc(gw_zeroed, 1)
            nc.gpsimd.memset(neg_half[:, :], -0.5).then_inc(setup_pool, 1)
            pool.wait_ge(setup_pool, 1)

            def inverse_root(n):
                pool.wait_ge(ln_var, n + 1)
                nc.gpsimd.tensor_tensor(rstd[:, n, :], vareps[:, n, :], neg_half[:, :], ALU.pow).then_inc(ln_rstd, 1)

            def low_gu(c, j, s):
                pool.wait_ge(guH_ready, s + 1)
                nc.gpsimd.tensor_tensor(guL[:, j, :], w_raw[:, c, 0:GU], guH[:, j, :], ALU.subtract).then_inc(guL_ready, 1)

            def low_dn(c, j, s):
                pool.wait_ge(dnH_ready, s + 1)
                nc.gpsimd.tensor_tensor(dnL[:, j, :], w_raw[:, c, GU:W_CHUNK], dnH[:, j, :],
                                        ALU.subtract).then_inc(dnL_ready, 1)

            def step(j, s, gu=None, dn=None):
                if gu is not None:
                    low_gu(gu, j, s + 2)
                if dn is not None:
                    low_dn(dn, 1 - j, s + 1)

            inverse_root(0)
            pool.wait_ge(wkvH_ready, 1)
            nc.gpsimd.tensor_tensor(wL[:, :, D_MODEL:2 * D_MODEL], w_att[:, :, D_MODEL:2 * D_MODEL],
                                    wH[:, :, D_MODEL:2 * D_MODEL], ALU.subtract).then_inc(wkL_ready, 1)
            pool.wait_ge(wqH_ready, 1)
            nc.gpsimd.tensor_tensor(wL[:, :, 0:D_MODEL], w_att[:, :, 0:D_MODEL], wH[:, :, 0:D_MODEL],
                                    ALU.subtract).then_inc(wqL_ready, 1)
            inverse_root(1)
            low_gu(0, 0, 0)
            low_gu(1, 1, 1)
            inverse_root(LN_ATT[0])
            inverse_root(LN_X1[0])
            low_dn(0, 0, 0)
            for s in range(8):
                step(s % 2, s, s + 2, s + 1)
                if s == 3:
                    inverse_root(LN_ATT[1])
                if s == 6:
                    inverse_root(LN_X1[1])
            with pool.Fori(8, CHUNKS - 3, 2) as c:
                for j in range(2):
                    step(j, c + j, c + (2 + j), c + (1 + j))
            step(0, CHUNKS - 2, 0, CHUNKS - 1)
            step(1, CHUNKS - 1, 1, 0)
            s0 = CHUNKS
            step(0, s0, 2, 1)
            step(1, s0 + 1, 3, 2)
            inverse_root(LN_MOE[0])
            with pool.Fori(2, CHUNKS - 3, 2) as c:
                for j in range(2):
                    step(j, c + (s0 + j), c + (2 + j), c + (1 + j))
            step(0, STEPS - 2, None, CHUNKS - 1)
            inverse_root(NORMS - 1)

        @block.tensor
        def _(pe):
            def product(dst, lhs, rhs, start=True, stop=True):
                return nc.tensor.matmul(dst, lhs, rhs, start=start, stop=stop)

            def split_product(dst, pairs, start=True, stop=True, low=None):
                n, last = 0, 3 * len(pairs) - 1
                for second in (0, 1):
                    if second and low is not None:
                        pe.wait_ge(*low)
                    for (lh, ll), right in pairs:
                        for a in ((lh, ll), (lh,))[second]:
                            mm = nc.tensor.matmul(dst, a, right[second], start=start and n == 0, stop=stop and n == last)
                            n += 1
                return mm

            def halves(front, back, b):
                return [(front, 2 * b + 1), (front, 2 * b + 2), (back, 2 * b + 1), (back, 2 * b + 2)]

            def turn(src, b, first, ready, psum_sem):
                for t in range(TILES):
                    pe.wait_ge(*ready[t])
                    for k in range(KD):
                        mm = nc.tensor.transpose(a_bank(b, first + k)[:, t * P:(t + 1) * P],
                                                 src[:, b, t, k * P:(k + 1) * P], ident)
                        if t == TILES - 1:
                            mm.then_inc(psum_sem, 1)

            def turn_rows(b):
                turn(y_sb, b, 0, [(o_ready, TILES * b + max(t, 1) + 1) for t in range(TILES)], oT_psum)

            def queries(b):
                pe.wait_ge(wqL_ready, 1)
                for m in range(KD):
                    r = slice(m * P, (m + 1) * P)
                    split_product(a_bank(b, 2 + m), [((wH[:, k, r], wL[:, k, r]), (zH[:, b, k, :], zL[:, b, k, :]))
                                                     for k in range(KD)]).then_inc(q_psum, 1)

            def keys_values(b, tiles):
                r = slice(D_MODEL, QKV)
                for t in tiles:
                    if t == 0:
                        pe.wait_ge(yL_ready, KD * (b + 1))
                        pe.wait_ge(wkL_ready, 1)
                    if t >= 2:
                        pe.wait_ge(kv_biased, TILES * b + t - 1)
                    c = slice(t * P, (t + 1) * P)
                    split_product(a_bank(b, t % 2), [((zH[:, b, k, c], zL[:, b, k, c]), (wH[:, k, r], wL[:, k, r]))
                                                     for k in range(KD)],
                                  low=(wvL_ready, 1) if t == 0 else None).then_inc(kv_psum, 1)

            def states(b):
                pe.wait_ge(kv_biased, TILES * (b + 1))
                for t in range(TILES):
                    pe.wait_ge(k_ready, TILES * b + t + 1)
                    for m in range(KD):
                        mm = product(a_bank(b, m)[:, 0:P + 1], kv[:, b, t, m, 0:P],
                                     kv[:, b, t, KD + m, :], t == 0, t == TILES - 1)
                mm.then_inc(state_psum, 1)

            def numerators(b):
                pe.wait_ge(state_ready, b + 1)
                pe.wait_ge(q_ready, KD * (b + 1))
                for t in range(TILES):
                    for m in range(KD):
                        mm = product(a_bank(b, t)[:, m * NUM_WIDTH:(m + 1) * NUM_WIDTH],
                                     qT[:, b, m, t * P:(t + 1) * P], state[:, b, m, :])
                    mm.then_inc(num_psum, 1)

            def projection(b, tiles=range(TILES)):
                pe.wait_ge(wo_in, 16)
                pe.wait_ge(oT_ready, KD * (b + 1))
                for t in tiles:
                    c = t * D_MODEL % 512 if ATT_BANKS[b].count(ATT_BANKS[b][t]) > 1 else 0
                    for k in range(KD):
                        mm = product(bank(ATT_BANKS[b][t])[:, c:c + D_MODEL],
                                     qT[:, b, k, t * P:(t + 1) * P], w_att[:, k, QKV:], k == 0, k == KD - 1)
                    if last_in_bank(ATT_BANKS, b, t):
                        mm.then_inc(att_psum, 1)

            def route(b):
                pe.wait_ge(setup_dve, 5)
                pe.wait_ge(zH_ready, KD * (b + 1))
                if b == 1:
                    pe.wait_ge(zL_ready, KD * (b + 1))
                split_product(bank(BANK_LOGITS),
                              [((gwH[:, k, :], gwL[:, k, :]), (zH[:, b, k, :], zL[:, b, k, :]))
                               for k in range(KD)], low=(zL_ready, KD * (b + 1))).then_inc(logits_psum, 1)

            def turn_logits(b):
                pe.wait_ge(logits_ready, b + 1)
                for t in range(TILES):
                    mm = nc.tensor.transpose(bank(BANK_TURNED_LOGITS)[:, t * EXPERTS:(t + 1) * EXPERTS],
                                             logits_T(b)[:, t * P:(t + 1) * P], ident[0:EXPERTS, 0:EXPERTS])
                mm.then_inc(turned_psum, 1)

            def turn_weights(b):
                pe.wait_ge(parts_ready, b + 1)
                dst = bank(BANK_COMB)[0:SPLITS * EXPERTS, :].bitcast(BF16)
                for t in range(TILES):
                    mm = nc.tensor.transpose(dst[:, t * P:(t + 1) * P],
                                             parts[:, b, t].rearrange("p s e -> p (s e)"), ident_bf[:, :])
                mm.then_inc(combT_psum, 1)

            def spread_weights(b, groups):
                pe.wait_ge(combT_ready, b + 1)
                for g in groups:
                    n = b * GROUPS + g
                    if g >= 2:
                        pe.wait_ge(weights_ready, n - 1)
                    product(bank(BANK_FREE + g % 2), sel[:, g * P:(g + 1) * P], combT[:, b, :]).then_inc(weights_psum, 1)

            def gate(b, j, s):
                if not (isinstance(s, int) and s < 2):
                    pe.wait_ge(silu_ready, s - 1)
                pe.wait_ge(guL_ready, s + 1)
                half_product(b, j, BANK_G, 0).then_inc(gate_psum, 1)

            def up(b, j, s, read=None):
                if not (isinstance(s, int) and s < 2):
                    pe.wait_ge(glu_ready if read is None else read, s - 1)
                half_product(b, j, BANK_U, KD * P).then_inc(up_psum, 1)

            def half_product(b, j, base, first):
                pairs = []
                for k in range(KD):
                    r = slice(first + k * P, first + (k + 1) * P)
                    pairs.append(((guH[:, j, r], guL[:, j, r]), (zH[:, b, k, :], zL[:, b, k, :])))
                return split_product(bank(base + j), pairs)

            def gate_up(b, j, s, read=None):
                gate(b, j, s)
                up(b, j, s, read)

            def down(j, s, start=False, stop=False):
                pe.wait_ge(dnL_ready, s + 1)
                pe.wait_ge(gluH_ready, s + 1)
                for m in range(KD):
                    for n, part in enumerate((dnH, dnL)):
                        product(bank(BANK_Y + m), part[:, j, m * P:(m + 1) * P], gluH[:, j, :], start and n == 0, False)
                pe.wait_ge(gluL_ready, s + 1)
                for m in range(KD):
                    mm = product(bank(BANK_Y + m), dnH[:, j, m * P:(m + 1) * P], gluL[:, j, :], False, stop)
                mm.then_inc(down_psum, 1)

            def turn_back(b):
                pe.wait_ge(outT_ready, KD * (b + 1))
                if b == 0:
                    pe.wait_ge(weights_ready, BATCHES * GROUPS)
                for t in range(TILES):
                    c = t * D_MODEL % 512 if MOE_BANKS[b].count(MOE_BANKS[b][t]) > 1 else 0
                    for k in range(KD):
                        mm = nc.tensor.transpose(bank(MOE_BANKS[b][t])[:, c + k * P:c + (k + 1) * P],
                                                 outT[:, b, k, t * P:(t + 1) * P], ident)
                    if last_in_bank(MOE_BANKS, b, t):
                        mm.then_inc(moe_psum, 1)

            def warm(count):
                for _ in range(count):
                    product(bank(7), zeros[:, 0:P], zeros[:, 0:512])

            pe.wait_ge(zeroed, 1)
            warm(WARM_START)
            pe.wait_ge(mats_in, 16)
            turn(y_sb, 0, 0, halves(y_front, y_back, 0), yT_psum)
            warm(WARM_Y)
            keys_values(0, range(TILES))
            queries(0)
            states(0)
            turn(y_sb, 1, 0, halves(y_front, y_back, 1), yT_psum)
            numerators(0)
            keys_values(1, range(1))
            turn_rows(0)
            keys_values(1, range(1, 2))
            projection(0)
            keys_values(1, range(2, TILES))
            queries(1)
            states(1)
            numerators(1)
            turn(y_sb, 0, 2, halves(z_front, z_back, 0), zT_psum)
            turn_rows(1)
            route(0)
            gate(0, 0, 0)
            turn_logits(0)
            up(0, 0, 0)
            gate_up(0, 1, 1)
            projection(1, range(1))
            turn_weights(0)
            projection(1, range(1, 2))
            pe.wait_ge(sel_in, 16)
            spread_weights(0, range(2))
            gate(0, 0, 2)
            up(0, 0, 2, first_product)
            spread_weights(0, range(2, 4))
            pe.wait_ge(silu_ready, 2)
            projection(1, range(2, TILES))
            pe.wait_ge(att_biased, TILES + 2)
            down(0, 0, start=True)
            spread_weights(0, range(4, 6))
            pe.wait_ge(att_biased, 2 * TILES)
            gate_up(0, 1, 3, first_product)
            spread_weights(0, range(6, 8))
            down(1, 1)
            down(0, 2)

            def turn_input():
                pe.wait_ge(weights_ready, GROUPS)
                turn(y_sb, 1, 2, halves(z_front, z_back, 1), zT_psum)

            beside = {
                8: turn_input,
                11: lambda: turn_logits(1),
            }
            for s in range(4, FIRST):
                gate_up(0, s % 2, s)
                if s == 11:
                    route(1)
                down((s - 1) % 2, s - 1)
                if s in beside:
                    beside[s]()
            with pe.Fori(FIRST, CHUNKS - 5, 2) as s:
                for j in range(2):
                    gate_up(0, j, s + j)
                    down(1 - j, s + (j - 1))
            turn_weights(1)
            for n, s in enumerate(range(CHUNKS - 4, CHUNKS)):
                gate_up(0, s % 2, s)
                spread_weights(1, range(2 * n, 2 * n + 2))
                down((s - 1) % 2, s - 1)

            s0 = CHUNKS
            gate_up(1, 0, s0)
            down(1, s0 - 1, stop=True)
            gate_up(1, 1, s0 + 1)
            turn_back(0)
            down(0, s0, start=True)
            with pe.Fori(2, CHUNKS - 1, 2) as c:
                for j in range(2):
                    gate_up(1, j, c + (s0 + j))
                    down(1 - j, c + (s0 + j - 1))
            down(1, STEPS - 1, stop=True)
            turn_back(1)

        @block.scalar
        def _(act):
            def out_turned(dst, b, first, psum_sem, ready):
                for k in range(KD):
                    act.wait_ge(psum_sem, KD * b + k + 1)
                    nc.scalar.copy(dst[:, b, k, :], a_bank(b, first + k)).then_inc(ready, 1)

            def ln_apply(n, dst, src, ready):
                act.wait_ge(shift_ready, n + 1)
                for t in BACK:
                    nc.scalar.activation(dst[:, t, :], src[t], ACT.Identity, bias=shift[:, n, t:t + 1],
                                         scale=rstd[:, n, t:t + 1]).then_inc(ready, 1)

            def queries(b):
                for m in range(KD):
                    act.wait_ge(q_psum, KD * b + m + 1)
                    nc.scalar.activation(qT[:, b, m, :], a_bank(b, 2 + m), ACT.Relu,
                                         bias=bq_sb[:, m:m + 1]).then_inc(q_ready, 1)

            def keys(b, tiles=range(TILES)):
                for t in tiles:
                    act.wait_ge(kv_biased, TILES * b + t + 1)
                    nc.scalar.activation(kv[:, b, t, 0:KD, 0:P], kv[:, b, t, 0:KD, 0:P], ACT.Relu,
                                         scale=cols[:, 0, t:t + 1]).then_inc(k_ready, 1)

            def split_gu(c, j, s):
                if not (isinstance(s, int) and s < 2):
                    act.wait_ge(up_psum, s - 1)
                nc.scalar.copy(guH[:, j, :], w_raw[:, c, 0:GU]).then_inc(guH_ready, 1)

            def split_dn(c, j, s):
                if not (isinstance(s, int) and s < 2):
                    act.wait_ge(down_psum, s - 1)
                nc.scalar.copy(dnH[:, j, :], w_raw[:, c, GU:W_CHUNK]).then_inc(dnH_ready, 1)

            def logits(b):
                act.wait_ge(logits_psum, b + 1)
                nc.scalar.copy(logits_T(b), bank(BANK_LOGITS)[0:EXPERTS, :]).then_inc(logits_ready, 1)

            def exponentials(b):
                act.wait_ge(shifted_ready, b + 1)
                nc.scalar.activation(expd[:, b], shifted[:, b], ACT.Exp).then_inc(exp_ready, 1)
                if b == 1:
                    nc.scalar.activation(scratch[:, :], neg_half[:, :], ACT.Silu)

            def weights_turned(b):
                act.wait_ge(combT_psum, b + 1)
                nc.scalar.copy(combT[:, b, :],
                               bank(BANK_COMB)[0:SPLITS * EXPERTS, 0:TOKENS // 2].bitcast(BF16)).then_inc(combT_ready, 1)

            def weights_spread(b, groups):
                for g in groups:
                    act.wait_ge(weights_psum, b * GROUPS + g + 1)
                    nc.scalar.copy(weight_tiles[b][:, g, :], bank(BANK_FREE + g % 2)).then_inc(weights_ready, 1)

            def silu(j, s):
                act.wait_ge(gate_psum, s + 1)
                if not (isinstance(s, int) and s < 2):
                    act.wait_ge(gluL_ready, s - 1)
                nc.scalar.activation(glu[:, j, :], bank(BANK_G + j), ACT.Silu).then_inc(silu_ready, 1)

            def high_glu(j, s):
                act.wait_ge(glu_ready, s + 1)
                if not (isinstance(s, int) and s < 2):
                    act.wait_ge(down_psum, s - 1)
                nc.scalar.copy(gluH[:, j, :], glu[:, j, :]).then_inc(gluH_ready, 1)

            def step(j, s, gu=None, dn=None, between=None):
                silu(j, s)
                if between is not None:
                    between()
                high_glu(j, s)
                if gu is not None:
                    split_gu(gu, j, s + 2)
                if dn is not None:
                    split_dn(dn, 1 - j, s + 1)

            def out_of_psum(b):
                act.wait_ge(down_psum, CHUNKS * (b + 1))
                nc.scalar.copy(outT[:, b, 0, :], bank(BANK_Y)).then_inc(outT_ready, 1)

            def result(b):
                ln_apply(LN_MOE[b], moe[:, b], moe_rows(b), moe_back)

            act.wait_ge(setup_pool, 1)
            nc.scalar.activation(scratch[:, :], neg_half[:, :], ACT.Relu)
            ln_apply(0, y_sb[:, 0], rows(x_sb, 0), y_back)
            act.wait_ge(wkv_in, 16)
            nc.scalar.copy(wH[:, :, D_MODEL:QKV], w_att[:, :, D_MODEL:QKV]).then_inc(wkvH_ready, 1)
            out_turned(zH, 0, 0, yT_psum, yH_ready)
            act.wait_ge(wq_in, 16)
            nc.scalar.copy(wH[:, :, 0:D_MODEL], w_att[:, :, 0:D_MODEL]).then_inc(wqH_ready, 1)
            act.wait_ge(bq_in, 16)
            act.wait_ge(cols_in, 16)
            keys(0, range(2))
            ln_apply(1, y_sb[:, 1], rows(x_sb, 1), y_back)
            keys(0, range(2, TILES))
            queries(0)
            out_turned(zH, 1, 0, yT_psum, yH_ready)
            act.wait_ge(ffn_in[0], 16)
            split_gu(0, 0, 0)
            out_turned(qT, 0, 0, oT_psum, oT_ready)
            keys(1, range(2))
            split_gu(1, 1, 1)
            ln_apply(LN_ATT[0], att[:, 0], rows(att, 0), att_back)
            keys(1, range(2, TILES))
            queries(1)
            ln_apply(LN_X1[0], y_sb[:, 0], rows(x1, 0), z_back)
            out_turned(zH, 0, 2, zT_psum, zH_ready)
            out_turned(qT, 1, 0, oT_psum, oT_ready)
            logits(0)
            split_dn(0, 0, 0)
            exponentials(0)
            split_gu(2, 0, 2)
            silu(0, 0)
            silu(1, 1)
            split_gu(3, 1, 3)
            weights_turned(0)
            weights_spread(0, range(2))
            high_glu(0, 0)
            split_dn(1, 1, 1)
            weights_spread(0, range(2, 4))
            high_glu(1, 1)
            silu(0, 2)
            weights_spread(0, range(4, 6))
            split_dn(2, 0, 2)
            high_glu(0, 2)
            act.wait_ge(ffn_in[1], 16)
            split_gu(4, 0, 4)
            silu(1, 3)
            split_dn(3, 1, 3)
            weights_spread(0, range(6, 8))
            high_glu(1, 3)
            split_gu(5, 1, 5)
            split_dn(4, 0, 4)
            between = {
                5: lambda: ln_apply(LN_ATT[1], att[:, 1], rows(att, 1), att_back),
                8: lambda: ln_apply(LN_X1[1], y_sb[:, 1], rows(x1, 1), z_back),
                9: lambda: out_turned(zH, 1, 2, zT_psum, zH_ready),
                11: lambda: logits(1),
                13: lambda: exponentials(1),
            }
            for s in range(4, FIRST):
                if (s + 2) % GROUP == 0:
                    act.wait_ge(ffn_in[(s + 2) // GROUP], 16)
                step(s % 2, s, s + 2, s + 1, between.get(s))
            for g in range((FIRST + 1) // GROUP + 1, W_GROUPS):
                act.wait_ge(ffn_in[g], 16)
            with act.Fori(FIRST, CHUNKS - 5, 2) as s:
                for j in range(2):
                    step(j, s + j, s + (2 + j), s + (1 + j))

            def weights_out(n):
                if n == 0:
                    weights_turned(1)
                weights_spread(1, range(2 * n, 2 * n + 2))

            for n, s in enumerate(range(CHUNKS - 4, CHUNKS)):
                step(s % 2, s, (s + 2) % CHUNKS, (s + 1) % CHUNKS, lambda: weights_out(n))

            s0 = CHUNKS
            step(0, s0, 2, 1, lambda: out_of_psum(0))
            step(1, s0 + 1, 3, 2)
            step(0, s0 + 2, 4, 3, lambda: result(0))
            step(1, s0 + 3, 5, 4)
            with act.Fori(4, CHUNKS - 3, 2) as c:
                for j in range(2):
                    step(j, c + (s0 + j), c + (2 + j), c + (1 + j))
            step(0, STEPS - 2, None, CHUNKS - 1)
            step(1, STEPS - 1)
            out_of_psum(1)
            result(1)

        @block.vector
        def _(dve):
            local = [0]

            def own(ins):
                ins.then_inc(dve_local, 1)
                local[0] += 1
                return local[0]

            stats_at = {}

            def take_stats(n, tiles, which, ready=None):
                for t in which:
                    if ready is not None:
                        ready(t)
                    stats_at[n] = own(nc.vector.bn_stats(stats[:, n, t, :], tiles[t]))

            def variance(n):
                dve.wait_ge(dve_local, stats_at[n])
                for t in range(TILES):
                    v = own(nc.vector.bn_aggr(mv[:, n, t, :], stats[:, n, t, :]))
                dve.wait_ge(dve_local, v)
                nc.vector.tensor_scalar(vareps[:, n, :], mv[:, n, :, 1], LN_EPS, None, ALU.add).then_inc(ln_var, 1)

            def ln_stats(n, tiles, ready=None):
                take_stats(n, tiles, range(TILES), ready)
                variance(n)

            def ln_apply(n, dst, src, ready):
                dve.wait_ge(ln_rstd, n + 1)
                nc.vector.scalar_tensor_tensor(shift[:, n, :], mv[:, n, :, 0], -1.0, rstd[:, n, :],
                                               ALU.mult, ALU.mult).then_inc(shift_ready, 1)
                for t in FRONT:
                    nc.vector.tensor_scalar(dst[:, t, :], src[t], mv[:, n, t, 0:1], rstd[:, n, t:t + 1],
                                            ALU.subtract, ALU.mult).then_inc(ready, 1)

            def wait_normed(front, back, b, t):
                dve.wait_ge(back if t in BACK else front, 2 * b + t % 2 + 1)

            def low_turned(b, first, high_ready, ready, which=range(KD)):
                for k in which:
                    dve.wait_ge(high_ready, KD * b + k + 1)
                    nc.vector.tensor_tensor(zL[:, b, k, :], a_bank(b, first + k), zH[:, b, k, :],
                                            ALU.subtract).then_inc(ready, 1)

            def keys_values(b, tiles):
                for t in tiles:
                    dve.wait_ge(kv_psum, TILES * b + t + 1)
                    nc.vector.tensor_tensor(kv[:, b, t, :, 0:P], a_bank(b, t % 2).rearrange("p (m e) -> p m e", e=P),
                                            bias_sb[:, 0:2 * D_MODEL].rearrange("p (m e) -> p m e", e=P),
                                            ALU.add).then_inc(kv_biased, 1)

            def states(b):
                dve.wait_ge(state_psum, b + 1)
                for m in range(KD):
                    own(nc.vector.tensor_tensor(state[:, b, m, 0:P], a_bank(b, m)[:, 0:P], head_mask, ALU.mult))
                own(nc.vector.tensor_scalar(state[:, b, 0, P:], head_cols, a_bank(b, 0)[:, P:P + 1], None, ALU.mult))
                nc.vector.tensor_scalar(state[:, b, 1, P:], head_cols, a_bank(b, 1)[:, P:P + 1],
                                        None, ALU.mult).then_inc(state_ready, 1)

            def numerator(b, t):
                return a_bank(b, t)[:, 0:KD * NUM_WIDTH].rearrange("p (m w) -> p m w", m=KD)

            def denominators(b, pair):
                for t in pair:
                    dve.wait_ge(num_psum, TILES * b + t + 1)
                    v = own(nc.vector.tensor_scalar(den[:, b, t], numerator(b, t)[:, :, P:], cols[:, 1, t:t + 1], None, ALU.add))
                return v

            def inverses(b, pair, v):
                dve.wait_ge(dve_local, v)
                r = slice(pair[0], pair[1] + 1)
                return own(nc.vector.reciprocal(rden[:, b, r], den[:, b, r]))

            def attention_rows(b, pair, v):
                dve.wait_ge(dve_local, v)
                for t in pair:
                    nc.vector.tensor_tensor(
                        y_sb[:, b, t, :].rearrange("p (m h e) -> p m h e", m=KD, e=D_HEAD),
                        numerator(b, t)[:, :, 0:P].rearrange("p m (h e) -> p m h e", e=D_HEAD),
                        rden[:, b, t].unsqueeze(3).to_broadcast([P, KD, HEADS_PART, D_HEAD]), ALU.mult).then_inc(o_ready, 1)

            def attention(b):
                first = inverses(b, (0, 1), denominators(b, (0, 1)))
                second = denominators(b, (2, 3))
                attention_rows(b, (0, 1), first)
                attention_rows(b, (2, 3), inverses(b, (2, 3), second))

            def projection(b, tiles):
                for t in tiles:
                    dve.wait_ge(att_psum, banks_done(ATT_BANKS, b, t))
                    c = t * D_MODEL % 512 if ATT_BANKS[b].count(ATT_BANKS[b][t]) > 1 else 0
                    nc.vector.tensor_tensor(att[:, b, t, :], bank(ATT_BANKS[b][t])[:, c:c + D_MODEL],
                                            bias_sb[:, 2 * D_MODEL:], ALU.add).then_inc(att_biased, 1)

            def norm_projection(b, project=False):
                def ready(t):
                    if project and t + 1 < TILES:
                        projection(b, range(t + 1, t + 2))
                    dve.wait_ge(att_biased, TILES * b + t + 1)

                if project:
                    projection(b, range(1))
                ln_stats(LN_ATT[b], rows(att, b), ready)

            def normalise(b):
                ln_apply(LN_ATT[b], att[:, b], rows(att, b), att_front)

            def residual(b, tiles):
                for t in tiles:
                    wait_normed(att_front, att_back, b, t)
                    nc.vector.tensor_tensor(x1[:, b, t, :], att[:, b, t, :], x_sb[:, b, t, :], ALU.add).then_inc(x1_ready, 1)

            def stats_x1(b, tiles):
                take_stats(LN_X1[b], rows(x1, b), tiles, lambda t: dve.wait_ge(x1_ready, TILES * b + t + 1))

            def expert_input(b):
                dve.wait_ge(oT_psum, KD * (b + 1))
                ln_apply(LN_X1[b], y_sb[:, b], rows(x1, b), z_front)

            def choose(b):
                dve.wait_ge(turned_psum, b + 1)
                logits = bank(BANK_TURNED_LOGITS)[:, 0:TILES * EXPERTS].rearrange("p (t e) -> p t e", t=TILES)
                for t in range(TILES):
                    v = own(nc.vector.max(top8[:, b, t, :], logits[:, t, :]))
                dve.wait_ge(dve_local, v)
                for t in range(TILES):
                    v = own(nc.vector.match_replace(others[:, b, t, :], top8[:, b, t, :], logits[:, t, :], LOWEST))
                largest = top8[:, b, :, 0:1].to_broadcast([P, TILES, EXPERTS])
                own(nc.vector.tensor_tensor(shifted[:, b, 0], logits, largest, ALU.subtract))
                dve.wait_ge(dve_local, v)
                nc.vector.tensor_tensor(shifted[:, b, 1], others[:, b], largest, ALU.subtract).then_inc(shifted_ready, 1)

            def expert_weights(b):
                dve.wait_ge(exp_ready, b + 1)
                v = own(nc.vector.tensor_tensor(chosen[:, b], expd[:, b, 0], expd[:, b, 1], ALU.subtract))
                dve.wait_ge(dve_local, v)
                v = own(nc.vector.tensor_reduce(wsum[:, b, :], chosen[:, b], AX_X, ALU.add))
                dve.wait_ge(dve_local, v)
                v = own(nc.vector.reciprocal(rsum[:, b, :], wsum[:, b, :]))
                dve.wait_ge(dve_local, v)
                v = own(nc.vector.tensor_tensor(comb[:, b], chosen[:, b],
                                                rsum[:, b, :].unsqueeze(2).to_broadcast([P, TILES, EXPERTS]), ALU.mult))
                dve.wait_ge(dve_local, v)
                left = comb[:, b]
                for n in range(SPLITS - 1):
                    v = own(nc.vector.tensor_copy(parts[:, b, :, n, :], left))
                    dve.wait_ge(dve_local, v)
                    v = own(nc.vector.tensor_tensor(rest[:, b, n], left, parts[:, b, :, n, :], ALU.subtract))
                    dve.wait_ge(dve_local, v)
                    left = rest[:, b, n]
                nc.vector.tensor_copy(parts[:, b, :, SPLITS - 1, :], left).then_inc(parts_ready, 1)

            def low_glu(j, s):
                dve.wait_ge(gluH_ready, s + 1)
                nc.vector.tensor_tensor(gluL[:, j, :], glu[:, j, :], gluH[:, j, :], ALU.subtract).then_inc(gluL_ready, 1)

            def step(b, g, j, s, between=None):
                dve.wait_ge(silu_ready, s + 1)
                nc.vector.tensor_tensor(glu[:, j, :], glu[:, j, :], weight_tiles[b][:, g, :],
                                        ALU.mult).then_inc(first_product, 1)
                dve.wait_ge(up_psum, s + 1)
                dve.wait_ge(first_product, s + 1)
                nc.vector.tensor_tensor(glu[:, j, :], bank(BANK_U + j), glu[:, j, :], ALU.mult).then_inc(glu_ready, 1)
                if between is not None:
                    between()
                low_glu(j, s)

            def times_up(j, s):
                dve.wait_ge(silu_ready, s + 1)
                dve.wait_ge(up_psum, s + 1)
                nc.vector.tensor_tensor(glu[:, j, :], bank(BANK_U + j), glu[:, j, :], ALU.mult).then_inc(first_product, 1)

            def times_weight(j, s):
                dve.wait_ge(first_product, s + 1)
                dve.wait_ge(weights_ready, s + 1)
                nc.vector.tensor_tensor(glu[:, j, :], glu[:, j, :], weight_tiles[0][:, s, :], ALU.mult).then_inc(glu_ready, 1)

            def steps(b, first, last):
                base = first - first % GROUPS
                with dve.Fori(first - base, last - base - 1, 2) as g:
                    for j in range(2):
                        step(b, g + j, j, g + (b * CHUNKS + base + j))

            def out_of_psum(b):
                dve.wait_ge(down_psum, CHUNKS * (b + 1))
                nc.vector.tensor_copy(outT[:, b, 1, :], bank(BANK_Y + 1)).then_inc(outT_ready, 1)

            def stats_output(b, tiles):
                take_stats(LN_MOE[b], moe_rows(b), tiles, lambda t: dve.wait_ge(moe_psum, banks_done(MOE_BANKS, b, t)))

            def normalise_output(b):
                ln_apply(LN_MOE[b], moe[:, b], moe_rows(b), moe_front)

            def result(b, tiles):
                for t in tiles:
                    wait_normed(moe_front, moe_back, b, t)
                    nc.vector.tensor_tensor(moe[:, b, t, :], moe[:, b, t, :], x1[:, b, t, :], ALU.add).then_inc(result_ready, 1)

            nc.vector.memset(zeros[:, :], 0.0).then_inc(zeroed, 1)
            for b in range(BATCHES):
                nc.vector.memset(kv[:, b, :, KD:, P:P + 1], 1.0).then_inc(setup_dve, 1)
            ln_stats(0, rows(x_sb, 0), lambda t: dve.wait_ge(x_in[0][t // 2], 16))
            dve.wait_ge(mats_in, 16)
            nc.vector.tensor_copy(ident_bf[:, :], ident).then_inc(setup_dve, 1)
            ln_apply(0, y_sb[:, 0], rows(x_sb, 0), y_front)
            dve.wait_ge(wkvH_ready, 1)
            nc.vector.tensor_tensor(wL[:, :, 2 * D_MODEL:QKV], w_att[:, :, 2 * D_MODEL:QKV], wH[:, :, 2 * D_MODEL:QKV],
                                    ALU.subtract).then_inc(wvL_ready, 1)
            low_turned(0, 0, yH_ready, yL_ready)
            ln_stats(1, rows(x_sb, 1), lambda t: dve.wait_ge(x_in[1][t // 2], 16))
            dve.wait_ge(bias_in, 16)
            dve.wait_ge(cols_in, 16)
            keys_values(0, range(2))
            ln_apply(1, y_sb[:, 1], rows(x_sb, 1), y_front)
            keys_values(0, range(2, TILES))
            dve.wait_ge(gw_in, 16)
            nc.vector.tensor_copy(gwH[:, :, :], gw_sb[:, :, :]).then_inc(setup_dve, 1)
            dve.wait_ge(setup_dve, 4)
            nc.vector.tensor_tensor(gwL[:, :, :], gw_sb[:, :, :], gwH[:, :, :], ALU.subtract).then_inc(setup_dve, 1)
            states(0)
            low_turned(1, 0, yH_ready, yL_ready)
            attention(0)
            keys_values(1, range(2))
            norm_projection(0, project=True)
            keys_values(1, range(2, TILES))
            normalise(0)
            residual(0, range(TILES))
            stats_x1(0, range(TILES))
            variance(LN_X1[0])
            states(1)
            expert_input(0)
            attention(1)
            low_turned(0, 2, zH_ready, zL_ready)
            choose(0)
            expert_weights(0)
            times_up(0, 0)
            times_up(1, 1)
            projection(1, range(2))
            times_weight(0, 0)
            low_glu(0, 0)
            projection(1, range(2, TILES))
            times_weight(1, 1)
            low_glu(1, 1)
            between = {
                3: lambda: take_stats(LN_ATT[1], rows(att, 1), FRONT),
                4: lambda: variance(LN_ATT[1]),
                5: lambda: normalise(1),
                6: lambda: residual(1, BACK),
                7: lambda: (stats_x1(1, BACK), variance(LN_X1[1])),
                8: lambda: expert_input(1),
                10: lambda: low_turned(1, 2, zH_ready, zL_ready, range(1)),
            }
            beside = {
                3: lambda: take_stats(LN_ATT[1], rows(att, 1), BACK),
                5: lambda: residual(1, FRONT),
                6: lambda: stats_x1(1, FRONT),
                10: lambda: low_turned(1, 2, zH_ready, zL_ready, range(1, KD)),
                12: lambda: choose(1),
                13: lambda: expert_weights(1),
            }
            for s in range(2, FIRST):
                step(0, s % GROUPS, s % 2, s, between.get(s))
                if s in beside:
                    beside[s]()
            steps(0, FIRST, 16)
            steps(0, 16, CHUNKS)
            step(1, 0, 0, CHUNKS, lambda: out_of_psum(0))
            step(1, 1, 1, CHUNKS + 1, lambda: stats_output(0, FRONT))
            stats_output(0, BACK)
            variance(LN_MOE[0])
            step(1, 2, 0, CHUNKS + 2, lambda: normalise_output(0))
            result(0, FRONT)
            step(1, 3, 1, CHUNKS + 3, lambda: result(0, BACK))
            steps(1, 4, 8)
            steps(1, 8, 16)
            steps(1, 16, CHUNKS)
            out_of_psum(1)
            stats_output(1, range(TILES))
            variance(LN_MOE[1])
            normalise_output(1)
            result(1, range(TILES))


def kernel(L0_attn_x, L0_attn_Wq, L0_attn_bq, L0_attn_Wk, L0_attn_bk, L0_attn_Wv, L0_attn_bv, L0_attn_Wo,
           L0_attn_bo, L0_ffn_gate_w, L0_ffn_gate_proj, L0_ffn_up_proj, L0_ffn_down_proj):
    import ml_dtypes as _ml
    import numpy as _np
    import concourse.bacc as _bacc
    from concourse import mybir as _mybir
    from concourse.bass_utils import run_bass_kernel_spmd as _run

    def rows_first(w):
        w = _np.asarray(w)
        return w.reshape(KD, P, w.shape[1]).transpose(1, 0, 2)

    def by_chunk(w):
        w = _np.asarray(w).reshape(GROUPS, 4, KD, P, CHUNKS // GROUPS, 32)
        return w.transpose(3, 4, 0, 2, 1, 5).reshape(P, CHUNKS, KD * P)

    down = _np.asarray(L0_ffn_down_proj).reshape(GROUPS, 4, CHUNKS // GROUPS, 32, D_MODEL)
    down = down.transpose(1, 3, 2, 0, 4).reshape(P, CHUNKS, D_MODEL)

    pos = _np.arange(TOKENS, dtype=_np.float32)
    decay = _np.exp(-pos / _np.float32(TOKENS)).reshape(TILES, P).T
    head = _np.arange(P) // D_HEAD
    mats = _np.concatenate([_np.eye(P), head[:, None] == head[None, :],
                            head[:, None] == _np.arange(HEADS_PART)[None, :]], axis=1).astype(_np.float32)
    sel = (_np.arange(SPLITS * EXPERTS)[:, None] % EXPERTS == _np.arange(GROUPS * P)[None, :] // 32).astype(_ml.bfloat16)

    arrays = {
        "x": L0_attn_x,
        "w_qkvo": _np.concatenate([rows_first(_np.asarray(w).T) for w in (L0_attn_Wq, L0_attn_Wk, L0_attn_Wv, L0_attn_Wo)], axis=2),
        "bias_q": _np.asarray(L0_attn_bq).reshape(KD, P).T,
        "bias_rows": _np.concatenate([_np.asarray(v) for v in (L0_attn_bk, L0_attn_bv, L0_attn_bo)]),
        "gate_w": rows_first(_np.asarray(L0_ffn_gate_w).T),
        "ffn_w": _np.concatenate([by_chunk(L0_ffn_gate_proj), by_chunk(L0_ffn_up_proj), down], axis=2),
        "c_cols": _np.stack([decay, _np.float32(1e-6) / decay], axis=1).astype(_np.float32),
        "c_mats": mats,
        "c_sel": sel,
    }
    nc = _bacc.Bacc("TRN2", target_bir_lowering=False, num_devices=1)
    feed, args = {}, []
    for name, a in arrays.items():
        a = _np.ascontiguousarray(a)
        feed[f"in_{name}"] = a
        args.append(nc.dram_tensor(f"in_{name}", a.shape, _mybir.dt.from_np(a.dtype), kind="ExternalInput").ap())
    out = nc.dram_tensor("out", (BATCHES, TOKENS, D_MODEL), F32, kind="ExternalOutput").ap()
    attention_moe_kernel(nc, *args, out)
    return _run(nc, [feed], core_ids=[0]).results[0]["out"]
```

```python
from contextlib import ExitStack

import concourse.bass as bass
from concourse import mybir

F32 = mybir.dt.float32
F32R = mybir.dt.float32r
BF16 = mybir.dt.bfloat16
ALU = mybir.AluOpType
ACT = mybir.ActivationFunctionType
AX_X = mybir.AxisListType.X

P = 128
BATCHES = 2
TILES = 4
TOKENS = TILES * P
D_MODEL = 256
KD = D_MODEL // P
HEADS = 16
D_HEAD = D_MODEL // HEADS
HEADS_PART = HEADS // KD
NUM_WIDTH = P + HEADS_PART
EXPERTS = 32
INTER = 96
TOP_K = 8
SPLITS = 3
CHUNKS = EXPERTS * INTER // P
GU = 2 * KD * P
W_CHUNK = GU + D_MODEL
STEPS = BATCHES * CHUNKS
GROUPS = EXPERTS // 4
W_GROUPS = 6
GROUP = CHUNKS // W_GROUPS
NORMS = 4 * BATCHES
LN_ATT, LN_X1, LN_MOE = (2, 4), (3, 5), (6, 7)
LN_EPS = 1e-5
QKV = 3 * D_MODEL
KV_POOL = 2
FRONT, BACK = (0, 1), (2, 3)
LOWEST = -3e38


def attention_moe_kernel(nc, x, w_qkvo, bias_q, bias_rows, gate_w, ffn_w, c_cols, c_mats, c_sel, out):
    with ExitStack() as ctx:
        def sb(name, shape, dt=F32):
            return ctx.enter_context(nc.sbuf_tensor(name, shape, dt))

        def sem(name):
            return ctx.enter_context(nc.semaphore(name))

        x_sb = sb("x_sb", [P, BATCHES, TILES, D_MODEL])
        w_att = sb("w_att", [P, KD, 4 * D_MODEL])
        bq_sb = sb("bq_sb", [P, KD])
        bias_sb = sb("bias_sb", [P, 3 * D_MODEL])
        gw_sb = sb("gw_sb", [P, KD, P])
        w_raw = sb("w_raw", [P, CHUNKS, W_CHUNK])
        cols = sb("cols", [P, 2, TILES])
        mats = sb("mats", [P, 2 * P + HEADS_PART])
        sel = sb("sel", [SPLITS * EXPERTS, GROUPS * P], BF16)
        ident = mats[:, 0:P]
        head_mask = mats[:, P:2 * P]
        head_cols = mats[:, 2 * P:2 * P + HEADS_PART]

        ident_bf = sb("ident_bf", [P, P], BF16)
        y_sb = sb("y_sb", [P, BATCHES, TILES, D_MODEL])
        turned = sb("turned", [P, 2, BATCHES, KD, TOKENS])
        qT = turned[:, 1]
        kv = sb("kv", [P, BATCHES, TILES, 2 * KD, P + 1])
        state = sb("state", [P, BATCHES, KD, NUM_WIDTH])
        den = sb("den", [P, BATCHES, TILES, KD, HEADS_PART])
        rden = sb("rden", [P, BATCHES, TILES, KD, HEADS_PART])
        att = sb("att", [P, BATCHES, TILES, D_MODEL])
        x1 = x_sb
        stats = sb("stats", [P, NORMS, TILES, 6])
        mv = sb("mv", [P, NORMS, TILES, 2])
        vareps = sb("vareps", [P, NORMS, TILES])
        rstd = sb("rstd", [P, NORMS, TILES])
        shift = sb("shift", [P, NORMS, TILES])
        neg_half = sb("neg_half", [P, TILES])
        scratch = sb("scratch", [P, TILES])
        zeros = sb("zeros", [P, 512], BF16)

        gwH = sb("gwH", [P, KD, P], F32R)
        gwL = sb("gwL", [P, KD, P], F32R)
        top8 = sb("top8", [P, BATCHES, TILES, TOP_K])
        others = sb("others", [P, BATCHES, TILES, EXPERTS])
        shifted = sb("shifted", [P, BATCHES, 2, TILES, EXPERTS])
        expd = sb("expd", [P, BATCHES, 2, TILES, EXPERTS])
        chosen = sb("chosen", [P, BATCHES, TILES, EXPERTS])
        wsum = sb("wsum", [P, BATCHES, TILES])
        rsum = sb("rsum", [P, BATCHES, TILES])
        comb = sb("comb", [P, BATCHES, TILES, EXPERTS])
        rest = sb("rest", [P, BATCHES, 2, TILES, EXPERTS])
        parts = sb("parts", [P, BATCHES, TILES, SPLITS, EXPERTS], BF16)
        combT = sb("combT", [SPLITS * EXPERTS, BATCHES, TOKENS], BF16)

        zH = sb("zH", [P, BATCHES, KD, TOKENS], F32R)
        zL = sb("zL", [P, BATCHES, KD, TOKENS], F32R)
        guH = sb("guH", [P, 2, GU], F32R)
        guL = sb("guL", [P, 2, GU], F32R)
        glu = sb("glu", [P, 2, TOKENS])
        split = sb("split", [P, 2 * KD * QKV], F32R)
        wH = split[:, 0:KD * QKV].rearrange("p (k c) -> p k c", k=KD)
        wL = split[:, KD * QKV:].rearrange("p (k c) -> p k c", k=KD)
        gluH = split[:, 0:2 * TOKENS].rearrange("p (j t) -> p j t", j=2)
        gluL = split[:, 2 * TOKENS:4 * TOKENS].rearrange("p (j t) -> p j t", j=2)
        dnH = split[:, 4 * TOKENS:4 * TOKENS + 2 * D_MODEL].rearrange("p (j c) -> p j c", j=2)
        dnL = split[:, 4 * TOKENS + 2 * D_MODEL:4 * TOKENS + 4 * D_MODEL].rearrange("p (j c) -> p j c", j=2)
        weight_tiles = [
            turned[:, :].rearrange("p a b k t -> p (a b k) t"),
            kv[:, :].rearrange("p b t m c -> p (b t m c)")[:, 0:GROUPS * TOKENS].rearrange("p (g t) -> p g t", g=GROUPS),
        ]
        outT = turned[:, 0]
        moe = att

        psum = ctx.enter_context(nc.psum_tensor("psum", [P, 8, 512], F32))

        def bank(n):
            return psum[:, n, :]

        def a_bank(b, n):
            return psum[:, 4 * b + n, :]

        def logits_T(b):
            return y_sb[0:EXPERTS, b].rearrange("p t d -> p (t d)")[:, 0:TOKENS]

        BANK_G, BANK_U, BANK_Y, BANK_FREE = 0, 2, 4, 6
        BANK_LOGITS, BANK_TURNED_LOGITS = (1, 6), (3, 7)
        BANK_COMB = 6
        BANK_TURNED_Y = 4
        ATT_BANKS = ((0, 1, 2, 3), (4, 4, 1, 1))
        MOE_BANKS = ((6, 6, 7, 7), (0, 1, 2, 3))

        WIDE = (True, False)

        def turned_half(first, wide, n):
            if wide:
                return psum[:, first + 2 * n:first + 2 * n + 2, 0:TOKENS // 2]
            return bank(first + n)

        def half_of(buf, b, wide, n):
            return buf[:, b, :, n * (TOKENS // 2):(n + 1) * (TOKENS // 2)] if wide else buf[:, b, n, :]

        def banks_done(banks, b, t):
            return (len(set(banks[0])) if b else 0) + len(set(banks[b][:t + 1]))

        def last_in_bank(banks, b, t):
            return t == TILES - 1 or banks[b][t + 1] != banks[b][t]

        FIRST = 14
        WARM_START, WARM_Y = 13, 3

        x_in = [[sem(f"x_in{b}_{n}") for n in range(2)] for b in range(BATCHES)]
        wq_in = sem("wq_in")
        wk_in = sem("wk_in")
        wv_in = sem("wv_in")
        wo_in = sem("wo_in")
        mats_in = sem("mats_in")
        bq_in = sem("bq_in")
        bias_in = sem("bias_in")
        cols_in = sem("cols_in")
        gw_in = sem("gw_in")
        sel_in = sem("sel_in")
        ffn_in = [sem(f"ffn_in{n}") for n in range(W_GROUPS)]
        out_done = sem("out_done")

        gw_zeroed = sem("gw_zeroed")
        zeroed = sem("zeroed")
        setup_dve = sem("setup_dve")
        setup_pool = sem("setup_pool")
        dve_local = sem("dve_local")
        ln_var = sem("ln_var")
        ln_rstd = sem("ln_rstd")
        shift_ready = sem("shift_ready")
        y_front = sem("y_front")
        y_back = sem("y_back")
        wqH_ready = sem("wqH_ready")
        wqL_ready = sem("wqL_ready")
        wkH_ready = sem("wkH_ready")
        wkL_ready = sem("wkL_ready")
        wvL_ready = sem("wvL_ready")
        yT_psum = sem("yT_psum")
        yH_ready = sem("yH_ready")
        yL_ready = sem("yL_ready")
        q_psum = sem("q_psum")
        q_ready = sem("q_ready")
        kv_psum = sem("kv_psum")
        kv_biased = sem("kv_biased")
        kv_biased_pool = sem("kv_biased_pool")
        kv_raw = sem("kv_raw")
        k_ready = sem("k_ready")
        state_psum = sem("state_psum")
        state_ready = sem("state_ready")
        num_psum = sem("num_psum")
        o_ready = sem("o_ready")
        oT_psum = sem("oT_psum")
        oT_ready = sem("oT_ready")
        att_psum = sem("att_psum")
        att_biased = sem("att_biased")
        att_front = sem("att_front")
        att_back = sem("att_back")
        x1_ready = sem("x1_ready")
        z_front = sem("z_front")
        z_back = sem("z_back")
        zT_psum = sem("zT_psum")
        zH_ready = sem("zH_ready")
        zL_ready = sem("zL_ready")
        logits_psum = sem("logits_psum")
        logits_ready = sem("logits_ready")
        turned_psum = sem("turned_psum")
        shifted_ready = sem("shifted_ready")
        exp_ready = sem("exp_ready")
        parts_ready = sem("parts_ready")
        combT_psum = sem("combT_psum")
        combT_ready = sem("combT_ready")
        weights_psum = sem("weights_psum")
        weights_ready = sem("weights_ready")

        guH_ready = sem("guH_ready")
        guL_ready = sem("guL_ready")
        dnH_ready = sem("dnH_ready")
        dnL_ready = sem("dnL_ready")
        gate_psum = sem("gate_psum")
        up_psum = sem("up_psum")
        silu_ready = sem("silu_ready")
        first_product = sem("first_product")
        glu_ready = sem("glu_ready")
        gluH_ready = sem("gluH_ready")
        gluL_ready = sem("gluL_ready")
        down_psum = sem("down_psum")
        last_psum = sem("last_psum")
        outT_first = sem("outT_first")
        outT_second = sem("outT_second")
        moe_psum = sem("moe_psum")
        moe_front = sem("moe_front")
        moe_back = sem("moe_back")
        result_ready = sem("result_ready")

        def rows(buf, b):
            return [buf[:, b, t, :] for t in range(TILES)]

        def moe_rows(b):
            two = len(set(MOE_BANKS[b])) < TILES
            return [bank(n)[:, (t % 2) * D_MODEL:(t % 2 + 1) * D_MODEL] if two else bank(n)[:, 0:D_MODEL]
                    for t, n in enumerate(MOE_BANKS[b])]

        block = ctx.enter_context(nc.Block())

        @block.sync
        def _(sp):
            def load_x(b):
                rows = x[b].rearrange("(t p) d -> p t d", p=P)
                for n in range(2):
                    tiles = slice(2 * n, 2 * n + 2)
                    sp.dma_start(x_sb[:, b, tiles], rows[:, tiles]).then_inc(x_in[b][n], 16)

            load_x(0)
            sp.dma_start(w_att[:, :, D_MODEL:2 * D_MODEL], w_qkvo[:, :, D_MODEL:2 * D_MODEL]).then_inc(wk_in, 16)
            sp.dma_start(mats[:, :], c_mats).then_inc(mats_in, 16)
            sp.dma_start(w_att[:, :, 2 * D_MODEL:QKV], w_qkvo[:, :, 2 * D_MODEL:QKV]).then_inc(wv_in, 16)
            sp.dma_start(bias_sb[:, :], bias_rows.partition_broadcast(P)).then_inc(bias_in, 16)
            sp.dma_start(cols[:, :, :], c_cols).then_inc(cols_in, 16)
            sp.dma_start(w_att[:, :, 0:D_MODEL], w_qkvo[:, :, 0:D_MODEL]).then_inc(wq_in, 16)
            sp.dma_start(bq_sb[:, :], bias_q).then_inc(bq_in, 16)
            load_x(1)
            sp.dma_start(w_att[:, :, QKV:], w_qkvo[:, :, QKV:]).then_inc(wo_in, 16)
            sp.wait_ge(gw_zeroed, 1)
            sp.dma_start(gw_sb[:, :, 0:EXPERTS], gate_w).then_inc(gw_in, 16)
            sp.dma_start(sel[:, :], c_sel).then_inc(sel_in, 16)
            for g in range(W_GROUPS):
                sp.dma_start(w_raw[:, g * GROUP:(g + 1) * GROUP, :],
                             ffn_w[:, g * GROUP:(g + 1) * GROUP, :]).then_inc(ffn_in[g], 16)
            for b in range(BATCHES):
                rows = out[b].rearrange("(t p) d -> p t d", p=P)
                for t in range(TILES):
                    sp.wait_ge(result_ready, TILES * b + t + 1)
                    sp.dma_start(rows[:, t, :], moe[:, b, t, :]).then_inc(out_done, 16)
            sp.wait_ge(out_done, 16 * BATCHES * TILES)

        @block.gpsimd
        def _(pool):
            nc.gpsimd.memset(gw_sb[:, :, :], 0.0).then_inc(gw_zeroed, 1)
            nc.gpsimd.memset(neg_half[:, :], -0.5).then_inc(setup_pool, 1)
            pool.wait_ge(setup_pool, 1)

            def inverse_root(n):
                pool.wait_ge(ln_var, n + 1)
                nc.gpsimd.tensor_tensor(rstd[:, n, :], vareps[:, n, :], neg_half[:, :], ALU.pow).then_inc(ln_rstd, 1)

            def low_gu(c, j, s):
                pool.wait_ge(guH_ready, s + 1)
                nc.gpsimd.tensor_tensor(guL[:, j, :], w_raw[:, c, 0:GU], guH[:, j, :], ALU.subtract).then_inc(guL_ready, 1)

            def low_dn(c, j, s):
                pool.wait_ge(dnH_ready, s + 1)
                nc.gpsimd.tensor_tensor(dnL[:, j, :], w_raw[:, c, GU:W_CHUNK], dnH[:, j, :],
                                        ALU.subtract).then_inc(dnL_ready, 1)

            def step(j, s, gu=None, dn=None):
                if gu is not None:
                    low_gu(gu, j, s + 2)
                if dn is not None:
                    low_dn(dn, 1 - j, s + 1)

            inverse_root(0)
            pool.wait_ge(wkH_ready, 1)
            nc.gpsimd.tensor_tensor(wL[:, :, D_MODEL:2 * D_MODEL], w_att[:, :, D_MODEL:2 * D_MODEL],
                                    wH[:, :, D_MODEL:2 * D_MODEL], ALU.subtract).then_inc(wkL_ready, 1)
            pool.wait_ge(wqH_ready, 1)
            nc.gpsimd.tensor_tensor(wL[:, :, 0:D_MODEL], w_att[:, :, 0:D_MODEL], wH[:, :, 0:D_MODEL],
                                    ALU.subtract).then_inc(wqL_ready, 1)
            inverse_root(1)
            low_gu(0, 0, 0)
            low_gu(1, 1, 1)
            inverse_root(LN_ATT[0])
            pool.wait_ge(kv_raw, 1)
            nc.gpsimd.tensor_tensor(kv[:, 1, KV_POOL, :, 0:P], kv[:, 1, KV_POOL, :, 0:P],
                                    bias_sb[:, 0:2 * D_MODEL].rearrange("p (m e) -> p m e", e=P),
                                    ALU.add).then_inc(kv_biased_pool, 1)
            inverse_root(LN_X1[0])
            low_dn(0, 0, 0)
            for s in range(8):
                step(s % 2, s, s + 2, s + 1)
                if s == 3:
                    inverse_root(LN_ATT[1])
                if s == 6:
                    inverse_root(LN_X1[1])
            with pool.Fori(8, CHUNKS - 3, 2) as c:
                for j in range(2):
                    step(j, c + j, c + (2 + j), c + (1 + j))
            step(0, CHUNKS - 2, 0, CHUNKS - 1)
            step(1, CHUNKS - 1, 1, 0)
            s0 = CHUNKS
            step(0, s0, 2, 1)
            step(1, s0 + 1, 3, 2)
            inverse_root(LN_MOE[0])
            with pool.Fori(2, CHUNKS - 3, 2) as c:
                for j in range(2):
                    step(j, c + (s0 + j), c + (2 + j), c + (1 + j))
            step(0, STEPS - 2, None, CHUNKS - 1)
            inverse_root(NORMS - 1)

        @block.tensor
        def _(pe):
            def product(dst, lhs, rhs, start=True, stop=True):
                return nc.tensor.matmul(dst, lhs, rhs, start=start, stop=stop)

            def split_product(dst, pairs, start=True, stop=True, low=None):
                n, last = 0, 3 * len(pairs) - 1
                for second in (0, 1):
                    if second and low is not None:
                        pe.wait_ge(*low)
                    for (lh, ll), right in pairs:
                        for a in ((lh, ll), (lh,))[second]:
                            mm = nc.tensor.matmul(dst, a, right[second], start=start and n == 0, stop=stop and n == last)
                            n += 1
                return mm

            def halves(front, back, b):
                return [(front, 2 * b + 1), (front, 2 * b + 2), (back, 2 * b + 1), (back, 2 * b + 2)]

            def turn(src, b, first, ready, psum_sem, wide=False):
                for t in range(TILES):
                    pe.wait_ge(*ready[t])
                    for k in range(KD):
                        n, c = (first + 2 * (t // 2) + k, t % 2) if wide else (first + k, t)
                        mm = nc.tensor.transpose(bank(n)[:, c * P:(c + 1) * P], src[:, b, t, k * P:(k + 1) * P], ident)
                        if t % 2 and k == KD - 1 if wide else t == TILES - 1:
                            mm.then_inc(psum_sem, 1)

            def turn_rows(b):
                read = (1, 1, 3, 3) if WIDE[b] else (1, 1, 2, 3)
                turn(y_sb, b, 4 * b, [(o_ready, TILES * b + n + 1) for n in read], oT_psum, WIDE[b])

            def queries(b, parts=range(KD)):
                pe.wait_ge(wqL_ready, 1)
                for m in parts:
                    r = slice(m * P, (m + 1) * P)
                    split_product(a_bank(b, 2 + m), [((wH[:, k, r], wL[:, k, r]), (zH[:, b, k, :], zL[:, b, k, :]))
                                                     for k in range(KD)]).then_inc(q_psum, 1)

            def keys_values(b, tiles):
                r = slice(D_MODEL, QKV)
                for t in tiles:
                    if t == 0:
                        pe.wait_ge(wkL_ready, 1)
                        pe.wait_ge(wvL_ready, 1)
                    if t >= 2:
                        pe.wait_ge(kv_biased, TILES * b + t - 1)
                    c = slice(t * P, (t + 1) * P)
                    if b == 1:
                        pe.wait_ge(yL_ready, KD * b + t // 2 + 1)
                    pe.wait_ge(yH_ready, KD * b + t // 2 + 1)
                    for k in range(KD):
                        for w in (wH, wL):
                            product(a_bank(b, t % 2), zH[:, b, k, c], w[:, k, r], k == 0 and w is wH, False)
                    pe.wait_ge(yL_ready, KD * b + t // 2 + 1)
                    for k in range(KD):
                        mm = product(a_bank(b, t % 2), zL[:, b, k, c], wH[:, k, r], False, k == KD - 1)
                    mm.then_inc(kv_psum, 1)

            def states(b):
                pe.wait_ge(kv_biased, TILES + (TILES - 1) * b)
                if b == 1:
                    pe.wait_ge(kv_raw, 1)
                for t in range(TILES):
                    pe.wait_ge(k_ready, TILES * b + t + 1)
                    for m in range(KD):
                        mm = product(a_bank(b, m)[:, 0:P + 1], kv[:, b, t, m, 0:P],
                                     kv[:, b, t, KD + m, :], t == 0, t == TILES - 1)
                mm.then_inc(state_psum, 1)

            def numerators(b):
                pe.wait_ge(state_ready, b + 1)
                for m, tiles in ((0, range(3)), (1, range(3)), (0, (3,)), (1, (3,))):
                    pe.wait_ge(q_ready, KD * b + m + 1)
                    for t in tiles:
                        mm = product(a_bank(b, t)[:, m * NUM_WIDTH:(m + 1) * NUM_WIDTH],
                                     qT[:, b, m, t * P:(t + 1) * P], state[:, b, m, :])
                        if m == KD - 1:
                            mm.then_inc(num_psum, 1)

            def projection(b, tiles=range(TILES)):
                pe.wait_ge(wo_in, 16)
                for t in tiles:
                    pe.wait_ge(oT_ready, KD * b + t // 2 + 1 if WIDE[b] else KD * (b + 1))
                    c = t * D_MODEL % 512 if ATT_BANKS[b].count(ATT_BANKS[b][t]) > 1 else 0
                    for k in range(KD):
                        mm = product(bank(ATT_BANKS[b][t])[:, c:c + D_MODEL],
                                     qT[:, b, k, t * P:(t + 1) * P], w_att[:, k, QKV:], k == 0, k == KD - 1)
                    if last_in_bank(ATT_BANKS, b, t):
                        mm.then_inc(att_psum, 1)

            def route(b):
                pe.wait_ge(setup_dve, 5)
                pe.wait_ge(zH_ready, KD * (b + 1))
                pe.wait_ge(zL_ready, KD * b + (1 if WIDE[b] else KD))
                split_product(bank(BANK_LOGITS[b]),
                              [((gwH[:, k, :], gwL[:, k, :]), (zH[:, b, k, :], zL[:, b, k, :]))
                               for k in range(KD)], low=(zL_ready, KD * (b + 1))).then_inc(logits_psum, 1)

            def turn_logits(b):
                pe.wait_ge(logits_ready, b + 1)
                for t in range(TILES):
                    mm = nc.tensor.transpose(bank(BANK_TURNED_LOGITS[b])[:, t * EXPERTS:(t + 1) * EXPERTS],
                                             logits_T(b)[:, t * P:(t + 1) * P], ident[0:EXPERTS, 0:EXPERTS])
                mm.then_inc(turned_psum, 1)

            def turn_weights(b):
                pe.wait_ge(parts_ready, b + 1)
                dst = bank(BANK_COMB)[0:SPLITS * EXPERTS, :].bitcast(BF16)
                for t in range(TILES):
                    mm = nc.tensor.transpose(dst[:, t * P:(t + 1) * P],
                                             parts[:, b, t].rearrange("p s e -> p (s e)"), ident_bf[:, :])
                mm.then_inc(combT_psum, 1)

            def spread_weights(b, groups):
                pe.wait_ge(combT_ready, b + 1)
                for g in groups:
                    n = b * GROUPS + g
                    if g >= 2:
                        pe.wait_ge(weights_ready, n - 1)
                    product(bank(BANK_FREE + g % 2), sel[:, g * P:(g + 1) * P], combT[:, b, :]).then_inc(weights_psum, 1)

            def gate(b, j, s):
                if not (isinstance(s, int) and s < 2):
                    pe.wait_ge(silu_ready, s - 1)
                pe.wait_ge(guL_ready, s + 1)
                half_product(b, j, BANK_G, 0).then_inc(gate_psum, 1)

            def up(b, j, s, read=None):
                if not (isinstance(s, int) and s < 2):
                    pe.wait_ge(glu_ready if read is None else read, s - 1)
                half_product(b, j, BANK_U, KD * P).then_inc(up_psum, 1)

            def half_product(b, j, base, first):
                pairs = []
                for k in range(KD):
                    r = slice(first + k * P, first + (k + 1) * P)
                    pairs.append(((guH[:, j, r], guL[:, j, r]), (zH[:, b, k, :], zL[:, b, k, :])))
                return split_product(bank(base + j), pairs)

            def gate_up(b, j, s, read=None):
                gate(b, j, s)
                up(b, j, s, read)

            def down(j, s, start=False, stop=False, last=False):
                pe.wait_ge(dnL_ready, s + 1)
                pe.wait_ge(gluH_ready, s + 1)
                for m in range(KD):
                    for n, part in enumerate((dnH, dnL)):
                        product(bank(BANK_Y + m), part[:, j, m * P:(m + 1) * P], gluH[:, j, :], start and n == 0, False)
                pe.wait_ge(gluL_ready, s + 1)
                for m in range(KD):
                    mm = product(bank(BANK_Y + m), dnH[:, j, m * P:(m + 1) * P], gluL[:, j, :], False, stop)
                    if last:
                        mm.then_inc(last_psum, 1)
                if not last:
                    mm.then_inc(down_psum, 1)

            def turn_back(b):
                if b == 0:
                    pe.wait_ge(weights_ready, BATCHES * GROUPS)
                for k in range(KD):
                    pe.wait_ge((outT_first, outT_second)[k], b + 1)
                    for t in range(TILES):
                        c = t * D_MODEL % 512 if MOE_BANKS[b].count(MOE_BANKS[b][t]) > 1 else 0
                        mm = nc.tensor.transpose(bank(MOE_BANKS[b][t])[:, c + k * P:c + (k + 1) * P],
                                                 outT[:, b, k, t * P:(t + 1) * P], ident)
                        if k == KD - 1 and last_in_bank(MOE_BANKS, b, t):
                            mm.then_inc(moe_psum, 1)

            def warm(count):
                for _ in range(count):
                    product(bank(0), zeros[:, 0:P], zeros[:, 0:512])

            pe.wait_ge(zeroed, 1)
            warm(WARM_START)
            pe.wait_ge(mats_in, 16)
            turn(y_sb, 0, BANK_TURNED_Y, halves(y_front, y_back, 0), yT_psum, wide=True)
            warm(WARM_Y)
            keys_values(0, range(TILES))
            queries(0, range(1))
            turn(y_sb, 1, BANK_TURNED_Y, halves(y_front, y_back, 1), yT_psum, wide=True)
            states(0)
            queries(0, range(1, KD))
            numerators(0)
            keys_values(1, range(1))
            turn_rows(0)
            projection(0)
            keys_values(1, range(1, 3))
            queries(1, range(1))
            keys_values(1, range(3, TILES))
            queries(1, range(1, KD))
            states(1)
            turn(y_sb, 0, 0, halves(z_front, z_back, 0), zT_psum, wide=True)
            numerators(1)
            route(0)
            gate(0, 0, 0)
            turn_logits(0)
            up(0, 0, 0)
            turn_rows(1)
            gate(0, 1, 1)
            pe.wait_ge(shifted_ready, 1)
            up(0, 1, 1)
            turn_weights(0)
            projection(1, range(2))
            pe.wait_ge(sel_in, 16)
            spread_weights(0, range(2))
            gate(0, 0, 2)
            up(0, 0, 2, first_product)
            spread_weights(0, range(2, 4))
            pe.wait_ge(silu_ready, 2)
            projection(1, range(2, TILES))
            pe.wait_ge(att_biased, TILES + 2)
            down(0, 0, start=True)
            spread_weights(0, range(4, 6))
            pe.wait_ge(att_biased, 2 * TILES)
            gate_up(0, 1, 3, first_product)
            spread_weights(0, range(6, 8))
            down(1, 1)
            down(0, 2)

            def turn_input():
                pe.wait_ge(weights_ready, GROUPS)
                turn(y_sb, 1, 6, halves(z_front, z_back, 1), zT_psum)

            beside = {
                8: turn_input,
                11: lambda: turn_logits(1),
            }
            for s in range(4, FIRST):
                gate_up(0, s % 2, s)
                if s == 11:
                    route(1)
                down((s - 1) % 2, s - 1)
                if s in beside:
                    beside[s]()
            with pe.Fori(FIRST, CHUNKS - 5, 2) as s:
                for j in range(2):
                    gate_up(0, j, s + j)
                    down(1 - j, s + (j - 1))
            turn_weights(1)
            for n, s in enumerate(range(CHUNKS - 4, CHUNKS)):
                gate_up(0, s % 2, s)
                spread_weights(1, range(2 * n, 2 * n + 2))
                down((s - 1) % 2, s - 1)

            s0 = CHUNKS
            gate_up(1, 0, s0)
            down(1, s0 - 1, stop=True)
            gate_up(1, 1, s0 + 1)
            turn_back(0)
            down(0, s0, start=True)
            with pe.Fori(2, CHUNKS - 3, 2) as c:
                for j in range(2):
                    gate_up(1, j, c + (s0 + j))
                    down(1 - j, c + (s0 + j - 1))
            gate_up(1, 0, STEPS - 2)
            gate_up(1, 1, STEPS - 1)
            down(1, STEPS - 3)
            down(0, STEPS - 2)
            down(1, STEPS - 1, stop=True, last=True)
            turn_back(1)

        @block.scalar
        def _(act):
            def out_turned(dst, b, first, psum_sem, ready, wide=False):
                for n in range(2):
                    act.wait_ge(psum_sem, KD * b + n + 1)
                    nc.scalar.copy(half_of(dst, b, wide, n), turned_half(first, wide, n)).then_inc(ready, 1)

            def center(n, dst, src, ready):
                act.wait_ge(shift_ready, n + 1)
                for t in BACK:
                    nc.scalar.activation(dst[:, t, :], src[t], ACT.Identity, bias=shift[:, n, t:t + 1]).then_inc(ready, 1)

            def ln_apply(n, dst, src, ready):
                act.wait_ge(shift_ready, n + 1)
                for t in BACK:
                    nc.scalar.activation(dst[:, t, :], src[t], ACT.Identity, bias=shift[:, n, t:t + 1],
                                         scale=rstd[:, n, t:t + 1]).then_inc(ready, 1)

            def queries(b, parts=range(KD)):
                for m in parts:
                    act.wait_ge(q_psum, KD * b + m + 1)
                    nc.scalar.activation(qT[:, b, m, :], a_bank(b, 2 + m), ACT.Relu,
                                         bias=bq_sb[:, m:m + 1]).then_inc(q_ready, 1)

            def keys(b, tiles=range(TILES)):
                for t in tiles:
                    if b == 1 and t == KV_POOL:
                        act.wait_ge(kv_biased_pool, 1)
                    else:
                        act.wait_ge(kv_biased, TILES * b + t + 1 - (b == 1 and t > KV_POOL))
                    nc.scalar.activation(kv[:, b, t, 0:KD, 0:P], kv[:, b, t, 0:KD, 0:P], ACT.Relu,
                                         scale=cols[:, 0, t:t + 1]).then_inc(k_ready, 1)

            def split_gu(c, j, s):
                if not (isinstance(s, int) and s < 2):
                    act.wait_ge(up_psum, s - 1)
                nc.scalar.copy(guH[:, j, :], w_raw[:, c, 0:GU]).then_inc(guH_ready, 1)

            def split_dn(c, j, s):
                if not (isinstance(s, int) and s < 2):
                    act.wait_ge(down_psum, s - 1)
                nc.scalar.copy(dnH[:, j, :], w_raw[:, c, GU:W_CHUNK]).then_inc(dnH_ready, 1)

            def logits(b):
                act.wait_ge(logits_psum, b + 1)
                nc.scalar.copy(logits_T(b), bank(BANK_LOGITS[b])[0:EXPERTS, :]).then_inc(logits_ready, 1)

            def exponentials(b):
                act.wait_ge(shifted_ready, b + 1)
                nc.scalar.activation(expd[:, b], shifted[:, b], ACT.Exp).then_inc(exp_ready, 1)
                if b == 1:
                    nc.scalar.activation(scratch[:, :], neg_half[:, :], ACT.Silu)

            def weights_turned(b):
                act.wait_ge(combT_psum, b + 1)
                nc.scalar.copy(combT[:, b, :],
                               bank(BANK_COMB)[0:SPLITS * EXPERTS, 0:TOKENS // 2].bitcast(BF16)).then_inc(combT_ready, 1)

            def weights_spread(b, groups):
                for g in groups:
                    act.wait_ge(weights_psum, b * GROUPS + g + 1)
                    nc.scalar.copy(weight_tiles[b][:, g, :], bank(BANK_FREE + g % 2)).then_inc(weights_ready, 1)

            def silu(j, s):
                act.wait_ge(gate_psum, s + 1)
                if not (isinstance(s, int) and s < 2):
                    act.wait_ge(gluL_ready, s - 1)
                nc.scalar.activation(glu[:, j, :], bank(BANK_G + j), ACT.Silu).then_inc(silu_ready, 1)

            def high_glu(j, s):
                act.wait_ge(glu_ready, s + 1)
                if not (isinstance(s, int) and s < 2):
                    act.wait_ge(down_psum, s - 1)
                nc.scalar.copy(gluH[:, j, :], glu[:, j, :]).then_inc(gluH_ready, 1)

            def step(j, s, gu=None, dn=None, between=None):
                silu(j, s)
                if between is not None:
                    between()
                high_glu(j, s)
                if gu is not None:
                    split_gu(gu, j, s + 2)
                if dn is not None:
                    split_dn(dn, 1 - j, s + 1)

            def out_of_psum(b):
                if b == 0:
                    act.wait_ge(down_psum, CHUNKS)
                else:
                    act.wait_ge(last_psum, 1)
                nc.scalar.copy(outT[:, b, 0, :], bank(BANK_Y)).then_inc(outT_first, 1)

            def center_output(b):
                center(LN_MOE[b], moe[:, b], moe_rows(b), moe_back)

            act.wait_ge(setup_pool, 1)
            nc.scalar.activation(scratch[:, :], neg_half[:, :], ACT.Relu)
            act.wait_ge(wk_in, 16)
            nc.scalar.copy(wH[:, :, D_MODEL:2 * D_MODEL], w_att[:, :, D_MODEL:2 * D_MODEL]).then_inc(wkH_ready, 1)
            ln_apply(0, y_sb[:, 0], rows(x_sb, 0), y_back)
            out_turned(zH, 0, BANK_TURNED_Y, yT_psum, yH_ready, wide=True)
            act.wait_ge(wq_in, 16)
            nc.scalar.copy(wH[:, :, 0:D_MODEL], w_att[:, :, 0:D_MODEL]).then_inc(wqH_ready, 1)
            act.wait_ge(bq_in, 16)
            act.wait_ge(cols_in, 16)
            keys(0, range(2))
            ln_apply(1, y_sb[:, 1], rows(x_sb, 1), y_back)
            keys(0, range(2, TILES))
            queries(0, range(1))
            out_turned(zH, 1, BANK_TURNED_Y, yT_psum, yH_ready, wide=True)
            queries(0, range(1, KD))
            act.wait_ge(ffn_in[0], 16)
            split_gu(0, 0, 0)
            out_turned(qT, 0, 0, oT_psum, oT_ready, WIDE[0])
            keys(1, range(1))
            split_gu(1, 1, 1)
            center(LN_ATT[0], att[:, 0], rows(att, 0), att_back)
            keys(1, range(1, 2))
            act.wait_ge(kv_psum, TILES + KV_POOL + 1)
            nc.scalar.copy(kv[:, 1, KV_POOL, :, 0:P],
                           a_bank(1, KV_POOL % 2).rearrange("p (m e) -> p m e", e=P)).then_inc(kv_raw, 1)
            keys(1, BACK)
            queries(1, range(1))
            ln_apply(LN_X1[0], y_sb[:, 0], rows(x1, 0), z_back)
            queries(1, range(1, KD))
            out_turned(zH, 0, 0, zT_psum, zH_ready, wide=True)
            logits(0)
            split_dn(0, 0, 0)
            exponentials(0)
            out_turned(qT, 1, 4, oT_psum, oT_ready, WIDE[1])
            split_gu(2, 0, 2)
            silu(0, 0)
            weights_turned(0)
            silu(1, 1)
            split_gu(3, 1, 3)
            weights_spread(0, range(2))
            high_glu(0, 0)
            split_dn(1, 1, 1)
            weights_spread(0, range(2, 4))
            high_glu(1, 1)
            silu(0, 2)
            weights_spread(0, range(4, 6))
            split_dn(2, 0, 2)
            high_glu(0, 2)
            act.wait_ge(ffn_in[1], 16)
            split_gu(4, 0, 4)
            silu(1, 3)
            split_dn(3, 1, 3)
            weights_spread(0, range(6, 8))
            high_glu(1, 3)
            split_gu(5, 1, 5)
            split_dn(4, 0, 4)
            between = {
                6: lambda: center(LN_ATT[1], att[:, 1], rows(att, 1), att_back),
                8: lambda: ln_apply(LN_X1[1], y_sb[:, 1], rows(x1, 1), z_back),
                9: lambda: out_turned(zH, 1, 6, zT_psum, zH_ready),
                11: lambda: logits(1),
                13: lambda: exponentials(1),
            }
            for s in range(4, FIRST):
                if (s + 2) % GROUP == 0:
                    act.wait_ge(ffn_in[(s + 2) // GROUP], 16)
                step(s % 2, s, s + 2, s + 1, between.get(s))
            for g in range((FIRST + 1) // GROUP + 1, W_GROUPS):
                act.wait_ge(ffn_in[g], 16)
            with act.Fori(FIRST, CHUNKS - 5, 2) as s:
                for j in range(2):
                    step(j, s + j, s + (2 + j), s + (1 + j))

            def weights_out(n):
                if n == 0:
                    weights_turned(1)
                weights_spread(1, range(2 * n, 2 * n + 2))

            for n, s in enumerate(range(CHUNKS - 4, CHUNKS)):
                step(s % 2, s, (s + 2) % CHUNKS, (s + 1) % CHUNKS, lambda: weights_out(n))

            s0 = CHUNKS
            step(0, s0, 2, 1, lambda: out_of_psum(0))
            step(1, s0 + 1, 3, 2)
            step(0, s0 + 2, 4, 3, lambda: center_output(0))
            step(1, s0 + 3, 5, 4)
            with act.Fori(4, CHUNKS - 3, 2) as c:
                for j in range(2):
                    step(j, c + (s0 + j), c + (2 + j), c + (1 + j))
            silu(0, STEPS - 2)
            high_glu(0, STEPS - 2)
            silu(1, STEPS - 1)
            split_dn(CHUNKS - 1, 1, STEPS - 1)
            high_glu(1, STEPS - 1)
            out_of_psum(1)
            center_output(1)

        @block.vector
        def _(dve):
            local = [0]

            def own(ins):
                ins.then_inc(dve_local, 1)
                local[0] += 1
                return local[0]

            stats_at = {}

            def take_stats(n, tiles, which, ready=None):
                for t in which:
                    if ready is not None:
                        ready(t)
                    stats_at[n, t] = own(nc.vector.bn_stats(stats[:, n, t, :], tiles[t]))

            def variance(n):
                for t in range(TILES):
                    dve.wait_ge(dve_local, stats_at[n, t])
                    v = own(nc.vector.bn_aggr(mv[:, n, t, :], stats[:, n, t, :]))
                dve.wait_ge(dve_local, v)
                nc.vector.tensor_scalar(vareps[:, n, :], mv[:, n, :, 1], LN_EPS, None, ALU.add).then_inc(ln_var, 1)

            def ln_stats(n, tiles, ready=None):
                take_stats(n, tiles, range(TILES), ready)
                variance(n)

            def ln_apply(n, dst, src, ready):
                dve.wait_ge(ln_rstd, n + 1)
                nc.vector.scalar_tensor_tensor(shift[:, n, :], mv[:, n, :, 0], -1.0, rstd[:, n, :],
                                               ALU.mult, ALU.mult).then_inc(shift_ready, 1)
                for t in FRONT:
                    nc.vector.tensor_scalar(dst[:, t, :], src[t], mv[:, n, t, 0:1], rstd[:, n, t:t + 1],
                                            ALU.subtract, ALU.mult).then_inc(ready, 1)

            def center(n, dst, src, ready):
                nc.vector.tensor_scalar(shift[:, n, :], mv[:, n, :, 0], -1.0, None, ALU.mult).then_inc(shift_ready, 1)
                for t in FRONT:
                    nc.vector.tensor_scalar(dst[:, t, :], src[t], mv[:, n, t, 0:1], None, ALU.subtract).then_inc(ready, 1)

            def add_normed(n, t, dst, src, other):
                dve.wait_ge(ln_rstd, n + 1)
                return nc.vector.scalar_tensor_tensor(dst, src, rstd[:, n, t:t + 1], other, ALU.mult, ALU.add)

            def wait_centered(front, back, b, t):
                dve.wait_ge(back if t in BACK else front, 2 * b + t % 2 + 1)

            def low_turned(b, first, high_ready, ready, which=range(KD), wide=False):
                for n in which:
                    dve.wait_ge(high_ready, KD * b + n + 1)
                    nc.vector.tensor_tensor(half_of(zL, b, wide, n), turned_half(first, wide, n), half_of(zH, b, wide, n),
                                            ALU.subtract).then_inc(ready, 1)

            def keys_values(b, tiles):
                for t in tiles:
                    dve.wait_ge(kv_psum, TILES * b + t + 1)
                    nc.vector.tensor_tensor(kv[:, b, t, :, 0:P], a_bank(b, t % 2).rearrange("p (m e) -> p m e", e=P),
                                            bias_sb[:, 0:2 * D_MODEL].rearrange("p (m e) -> p m e", e=P),
                                            ALU.add).then_inc(kv_biased, 1)

            def states(b):
                dve.wait_ge(state_psum, b + 1)
                for m in range(KD):
                    own(nc.vector.tensor_tensor(state[:, b, m, 0:P], a_bank(b, m)[:, 0:P], head_mask, ALU.mult))
                own(nc.vector.tensor_scalar(state[:, b, 0, P:], head_cols, a_bank(b, 0)[:, P:P + 1], None, ALU.mult))
                nc.vector.tensor_scalar(state[:, b, 1, P:], head_cols, a_bank(b, 1)[:, P:P + 1],
                                        None, ALU.mult).then_inc(state_ready, 1)

            def numerator(b, t):
                return a_bank(b, t)[:, 0:KD * NUM_WIDTH].rearrange("p (m w) -> p m w", m=KD)

            def denominators(b, pair):
                for t in pair:
                    dve.wait_ge(num_psum, TILES * b + t + 1)
                    v = own(nc.vector.tensor_scalar(den[:, b, t], numerator(b, t)[:, :, P:], cols[:, 1, t:t + 1], None, ALU.add))
                return v

            def inverses(b, pair, v):
                dve.wait_ge(dve_local, v)
                r = slice(pair[0], pair[1] + 1)
                return own(nc.vector.reciprocal(rden[:, b, r], den[:, b, r]))

            def attention_rows(b, pair, v):
                dve.wait_ge(dve_local, v)
                for t in pair:
                    nc.vector.tensor_tensor(
                        y_sb[:, b, t, :].rearrange("p (m h e) -> p m h e", m=KD, e=D_HEAD),
                        numerator(b, t)[:, :, 0:P].rearrange("p m (h e) -> p m h e", e=D_HEAD),
                        rden[:, b, t].unsqueeze(3).to_broadcast([P, KD, HEADS_PART, D_HEAD]), ALU.mult).then_inc(o_ready, 1)

            def attention(b):
                first = inverses(b, (0, 1), denominators(b, (0, 1)))
                second = denominators(b, (2, 3))
                attention_rows(b, (0, 1), first)
                attention_rows(b, (2, 3), inverses(b, (2, 3), second))

            def projection(b, tiles):
                for t in tiles:
                    dve.wait_ge(att_psum, banks_done(ATT_BANKS, b, t))
                    c = t * D_MODEL % 512 if ATT_BANKS[b].count(ATT_BANKS[b][t]) > 1 else 0
                    nc.vector.tensor_tensor(att[:, b, t, :], bank(ATT_BANKS[b][t])[:, c:c + D_MODEL],
                                            bias_sb[:, 2 * D_MODEL:], ALU.add).then_inc(att_biased, 1)

            def norm_projection(b, project=False):
                def ready(t):
                    if project and t + 1 < TILES:
                        projection(b, range(t + 1, t + 2))
                    dve.wait_ge(att_biased, TILES * b + t + 1)

                if project:
                    projection(b, range(1))
                ln_stats(LN_ATT[b], rows(att, b), ready)

            def center_projection(b):
                center(LN_ATT[b], att[:, b], rows(att, b), att_front)

            def residual(b, tiles):
                for t in tiles:
                    wait_centered(att_front, att_back, b, t)
                    add_normed(LN_ATT[b], t, x1[:, b, t, :], att[:, b, t, :], x_sb[:, b, t, :]).then_inc(x1_ready, 1)

            def stats_x1(b, tiles):
                take_stats(LN_X1[b], rows(x1, b), tiles, lambda t: dve.wait_ge(x1_ready, TILES * b + t + 1))

            def expert_input(b):
                dve.wait_ge(oT_psum, KD * (b + 1))
                ln_apply(LN_X1[b], y_sb[:, b], rows(x1, b), z_front)

            def choose(b):
                dve.wait_ge(turned_psum, b + 1)
                logits = bank(BANK_TURNED_LOGITS[b])[:, 0:TILES * EXPERTS].rearrange("p (t e) -> p t e", t=TILES)
                for t in range(TILES):
                    v = own(nc.vector.max(top8[:, b, t, :], logits[:, t, :]))
                dve.wait_ge(dve_local, v)
                for t in range(TILES):
                    v = own(nc.vector.match_replace(others[:, b, t, :], top8[:, b, t, :], logits[:, t, :], LOWEST))
                largest = top8[:, b, :, 0:1].to_broadcast([P, TILES, EXPERTS])
                own(nc.vector.tensor_tensor(shifted[:, b, 0], logits, largest, ALU.subtract))
                dve.wait_ge(dve_local, v)
                nc.vector.tensor_tensor(shifted[:, b, 1], others[:, b], largest, ALU.subtract).then_inc(shifted_ready, 1)

            comb_at = {}

            def softmax(b):
                dve.wait_ge(exp_ready, b + 1)
                v = own(nc.vector.tensor_tensor(chosen[:, b], expd[:, b, 0], expd[:, b, 1], ALU.subtract))
                dve.wait_ge(dve_local, v)
                v = own(nc.vector.tensor_reduce(wsum[:, b, :], chosen[:, b], AX_X, ALU.add))
                dve.wait_ge(dve_local, v)
                v = own(nc.vector.reciprocal(rsum[:, b, :], wsum[:, b, :]))
                dve.wait_ge(dve_local, v)
                v = own(nc.vector.tensor_tensor(comb[:, b], chosen[:, b],
                                                rsum[:, b, :].unsqueeze(2).to_broadcast([P, TILES, EXPERTS]), ALU.mult))
                comb_at[b] = v

            def split_weights(b):
                dve.wait_ge(dve_local, comb_at[b])
                left = comb[:, b]
                for n in range(SPLITS - 1):
                    v = own(nc.vector.tensor_copy(parts[:, b, :, n, :], left))
                    dve.wait_ge(dve_local, v)
                    v = own(nc.vector.tensor_tensor(rest[:, b, n], left, parts[:, b, :, n, :], ALU.subtract))
                    dve.wait_ge(dve_local, v)
                    left = rest[:, b, n]
                nc.vector.tensor_copy(parts[:, b, :, SPLITS - 1, :], left).then_inc(parts_ready, 1)

            def low_glu(j, s):
                dve.wait_ge(gluH_ready, s + 1)
                nc.vector.tensor_tensor(gluL[:, j, :], glu[:, j, :], gluH[:, j, :], ALU.subtract).then_inc(gluL_ready, 1)

            def step(b, g, j, s, between=None):
                dve.wait_ge(silu_ready, s + 1)
                nc.vector.tensor_tensor(glu[:, j, :], glu[:, j, :], weight_tiles[b][:, g, :],
                                        ALU.mult).then_inc(first_product, 1)
                dve.wait_ge(up_psum, s + 1)
                dve.wait_ge(first_product, s + 1)
                nc.vector.tensor_tensor(glu[:, j, :], bank(BANK_U + j), glu[:, j, :], ALU.mult).then_inc(glu_ready, 1)
                if between is not None:
                    between()
                low_glu(j, s)

            def times_up(j, s):
                dve.wait_ge(silu_ready, s + 1)
                dve.wait_ge(up_psum, s + 1)
                nc.vector.tensor_tensor(glu[:, j, :], bank(BANK_U + j), glu[:, j, :], ALU.mult).then_inc(first_product, 1)

            def times_weight(j, s):
                dve.wait_ge(first_product, s + 1)
                dve.wait_ge(weights_ready, s + 1)
                nc.vector.tensor_tensor(glu[:, j, :], glu[:, j, :], weight_tiles[0][:, s, :], ALU.mult).then_inc(glu_ready, 1)

            def steps(b, first, last):
                base = first - first % GROUPS
                with dve.Fori(first - base, last - base - 1, 2) as g:
                    for j in range(2):
                        step(b, g + j, j, g + (b * CHUNKS + base + j))

            def out_of_psum(b):
                if b == 0:
                    dve.wait_ge(down_psum, CHUNKS)
                else:
                    dve.wait_ge(last_psum, 2)
                nc.vector.tensor_copy(outT[:, b, 1, :], bank(BANK_Y + 1)).then_inc(outT_second, 1)

            def stats_output(b, tiles):
                take_stats(LN_MOE[b], moe_rows(b), tiles, lambda t: dve.wait_ge(moe_psum, banks_done(MOE_BANKS, b, t)))

            def center_output(b):
                center(LN_MOE[b], moe[:, b], moe_rows(b), moe_front)

            def result(b, tiles):
                for t in tiles:
                    wait_centered(moe_front, moe_back, b, t)
                    add_normed(LN_MOE[b], t, moe[:, b, t, :], moe[:, b, t, :], x1[:, b, t, :]).then_inc(result_ready, 1)

            nc.vector.memset(zeros[:, :], 0.0).then_inc(zeroed, 1)
            for b in range(BATCHES):
                nc.vector.memset(kv[:, b, :, KD:, P:P + 1], 1.0).then_inc(setup_dve, 1)
            ln_stats(0, rows(x_sb, 0), lambda t: dve.wait_ge(x_in[0][t // 2], 16))
            ln_apply(0, y_sb[:, 0], rows(x_sb, 0), y_front)
            dve.wait_ge(wv_in, 16)
            v_cols = slice(2 * D_MODEL, QKV)
            v = own(nc.vector.tensor_copy(wH[:, :, v_cols], w_att[:, :, v_cols]))
            dve.wait_ge(dve_local, v)
            nc.vector.tensor_tensor(wL[:, :, v_cols], w_att[:, :, v_cols], wH[:, :, v_cols],
                                    ALU.subtract).then_inc(wvL_ready, 1)
            low_turned(0, BANK_TURNED_Y, yH_ready, yL_ready, wide=True)
            def x1_here(t):
                dve.wait_ge(x_in[1][t // 2], 16)

            take_stats(1, rows(x_sb, 1), FRONT, x1_here)
            dve.wait_ge(bias_in, 16)
            keys_values(0, range(1))
            take_stats(1, rows(x_sb, 1), BACK, x1_here)
            keys_values(0, range(1, 2))
            variance(1)
            ln_apply(1, y_sb[:, 1], rows(x_sb, 1), y_front)
            keys_values(0, range(2, TILES))
            dve.wait_ge(mats_in, 16)
            nc.vector.tensor_copy(ident_bf[:, :], ident).then_inc(setup_dve, 1)
            dve.wait_ge(gw_in, 16)
            nc.vector.tensor_copy(gwH[:, :, :], gw_sb[:, :, :]).then_inc(setup_dve, 1)
            dve.wait_ge(setup_dve, 4)
            nc.vector.tensor_tensor(gwL[:, :, :], gw_sb[:, :, :], gwH[:, :, :], ALU.subtract).then_inc(setup_dve, 1)
            low_turned(1, BANK_TURNED_Y, yH_ready, yL_ready, range(1), wide=True)
            states(0)
            dve.wait_ge(cols_in, 16)
            attention(0)
            low_turned(1, BANK_TURNED_Y, yH_ready, yL_ready, range(1, 2), wide=True)
            keys_values(1, range(1))
            norm_projection(0, project=True)
            center_projection(0)
            keys_values(1, range(1, 2))
            residual(0, range(TILES))
            stats_x1(0, range(TILES))
            variance(LN_X1[0])
            keys_values(1, range(3, TILES))
            expert_input(0)
            states(1)
            low_turned(0, 0, zH_ready, zL_ready, wide=True)
            attention(1)
            choose(0)
            softmax(0)
            split_weights(0)
            times_up(0, 0)
            times_up(1, 1)
            projection(1, range(2))
            times_weight(0, 0)
            low_glu(0, 0)
            times_weight(1, 1)
            low_glu(1, 1)
            projection(1, range(2, TILES))
            between = {
                3: lambda: take_stats(LN_ATT[1], rows(att, 1), FRONT),
                4: lambda: variance(LN_ATT[1]),
                5: lambda: center_projection(1),
                6: lambda: residual(1, BACK),
                7: lambda: (stats_x1(1, BACK), variance(LN_X1[1])),
                8: lambda: expert_input(1),
                10: lambda: low_turned(1, 6, zH_ready, zL_ready, range(1)),
                13: lambda: softmax(1),
            }
            beside = {
                3: lambda: take_stats(LN_ATT[1], rows(att, 1), BACK),
                5: lambda: residual(1, FRONT),
                6: lambda: stats_x1(1, FRONT),
                10: lambda: low_turned(1, 6, zH_ready, zL_ready, range(1, KD)),
                12: lambda: choose(1),
                13: lambda: split_weights(1),
            }
            for s in range(2, FIRST):
                step(0, s % GROUPS, s % 2, s, between.get(s))
                if s in beside:
                    beside[s]()
            steps(0, FIRST, 16)
            steps(0, 16, CHUNKS)
            step(1, 0, 0, CHUNKS, lambda: out_of_psum(0))
            step(1, 1, 1, CHUNKS + 1, lambda: stats_output(0, FRONT))
            stats_output(0, BACK)
            variance(LN_MOE[0])
            center_output(0)
            step(1, 2, 0, CHUNKS + 2, lambda: result(0, FRONT))
            step(1, 3, 1, CHUNKS + 3, lambda: result(0, BACK))
            steps(1, 4, 8)
            steps(1, 8, 16)
            steps(1, 16, CHUNKS)
            out_of_psum(1)
            stats_output(1, range(TILES))
            variance(LN_MOE[1])
            center_output(1)
            result(1, range(TILES))


def kernel(L0_attn_x, L0_attn_Wq, L0_attn_bq, L0_attn_Wk, L0_attn_bk, L0_attn_Wv, L0_attn_bv, L0_attn_Wo,
           L0_attn_bo, L0_ffn_gate_w, L0_ffn_gate_proj, L0_ffn_up_proj, L0_ffn_down_proj):
    import ml_dtypes as _ml
    import numpy as _np
    import concourse.bacc as _bacc
    from concourse import mybir as _mybir
    from concourse.bass_utils import run_bass_kernel_spmd as _run

    def rows_first(w):
        w = _np.asarray(w)
        return w.reshape(KD, P, w.shape[1]).transpose(1, 0, 2)

    def by_chunk(w):
        w = _np.asarray(w).reshape(GROUPS, 4, KD, P, CHUNKS // GROUPS, 32)
        return w.transpose(3, 4, 0, 2, 1, 5).reshape(P, CHUNKS, KD * P)

    down = _np.asarray(L0_ffn_down_proj).reshape(GROUPS, 4, CHUNKS // GROUPS, 32, D_MODEL)
    down = down.transpose(1, 3, 2, 0, 4).reshape(P, CHUNKS, D_MODEL)

    pos = _np.arange(TOKENS, dtype=_np.float32)
    decay = _np.exp(-pos / _np.float32(TOKENS)).reshape(TILES, P).T
    head = _np.arange(P) // D_HEAD
    mats = _np.concatenate([_np.eye(P), head[:, None] == head[None, :],
                            head[:, None] == _np.arange(HEADS_PART)[None, :]], axis=1).astype(_np.float32)
    sel = (_np.arange(SPLITS * EXPERTS)[:, None] % EXPERTS == _np.arange(GROUPS * P)[None, :] // 32).astype(_ml.bfloat16)

    arrays = {
        "x": L0_attn_x,
        "w_qkvo": _np.concatenate([rows_first(_np.asarray(w).T) for w in (L0_attn_Wq, L0_attn_Wk, L0_attn_Wv, L0_attn_Wo)], axis=2),
        "bias_q": _np.asarray(L0_attn_bq).reshape(KD, P).T,
        "bias_rows": _np.concatenate([_np.asarray(v) for v in (L0_attn_bk, L0_attn_bv, L0_attn_bo)]),
        "gate_w": rows_first(_np.asarray(L0_ffn_gate_w).T),
        "ffn_w": _np.concatenate([by_chunk(L0_ffn_gate_proj), by_chunk(L0_ffn_up_proj), down], axis=2),
        "c_cols": _np.stack([decay, _np.float32(1e-6) / decay], axis=1).astype(_np.float32),
        "c_mats": mats,
        "c_sel": sel,
    }
    nc = _bacc.Bacc("TRN2", target_bir_lowering=False, num_devices=1)
    feed, args = {}, []
    for name, a in arrays.items():
        a = _np.ascontiguousarray(a)
        feed[f"in_{name}"] = a
        args.append(nc.dram_tensor(f"in_{name}", a.shape, _mybir.dt.from_np(a.dtype), kind="ExternalInput").ap())
    out = nc.dram_tensor("out", (BATCHES, TOKENS, D_MODEL), F32, kind="ExternalOutput").ap()
    attention_moe_kernel(nc, *args, out)
    return _run(nc, [feed], core_ids=[0]).results[0]["out"]
```
